# Optimizing a Trainium2 kernel written in Bass

```python
import numpy as np
import jax
import jax.numpy as jnp

def _softmax(x, axis=-1):
    return jax.nn.softmax(x, axis=axis)

def _gelu(x):
    return jax.nn.gelu(x, approximate=True)

def _silu(x):
    return jax.nn.silu(x)

def _sigmoid(x):
    return jax.nn.sigmoid(x)

def _layernorm(x, axis=-1, eps=1e-05):
    m = jnp.mean(x, axis=axis, keepdims=True)
    v = jnp.var(x, axis=axis, keepdims=True)
    return (x - m) / jnp.sqrt(v + eps)

def _scatter_add(tgt, idx, src, axis=0):
    return tgt.at[idx].add(src)

def _segment_sum(src, seg, n):
    return jax.ops.segment_sum(src, seg, n)
kernel_name = 'mk_dlrm_tower_d1_rec_r8_9929d6'

def setup_inputs(seed: int=0):
    np.random.seed(seed)
    _w = jnp.asarray

    def _rec_inputs():
        import jax
        import jax.numpy as jnp
        _tk = jax.random.key(seed)
        dense_ctx = jax.random.normal(jax.random.fold_in(_tk, 190), (1024, 16), jnp.float32)
        ids = jnp.stack([jax.random.randint(jax.random.fold_in(_tk, 200 + f), (1024,), 0, v, jnp.int32) for f, v in enumerate([12500, 1250, 125000, 12500, 12500, 12500, 1000, 125000, 125000, 12500, 1000, 1000, 1000, 1000, 1000, 1250, 125000, 1250, 1000, 125000, 125000, 125000, 1000, 1250, 1250, 12500, 1250, 1250, 1000, 1000, 1000, 1250])], axis=1)
        tbl_0 = 0.05 * jax.random.normal(jax.random.fold_in(_tk, 500 + 0), (12500, 32), jnp.float32)
        tbl_1 = 0.05 * jax.random.normal(jax.random.fold_in(_tk, 500 + 1), (1250, 32), jnp.float32)
        tbl_2 = 0.05 * jax.random.normal(jax.random.fold_in(_tk, 500 + 2), (125000, 32), jnp.float32)
        tbl_3 = 0.05 * jax.random.normal(jax.random.fold_in(_tk, 500 + 3), (12500, 32), jnp.float32)
        tbl_4 = 0.05 * jax.random.normal(jax.random.fold_in(_tk, 500 + 4), (12500, 32), jnp.float32)
        tbl_5 = 0.05 * jax.random.normal(jax.random.fold_in(_tk, 500 + 5), (12500, 32), jnp.float32)
        tbl_6 = 0.05 * jax.random.normal(jax.random.fold_in(_tk, 500 + 6), (1000, 32), jnp.float32)
        tbl_7 = 0.05 * jax.random.normal(jax.random.fold_in(_tk, 500 + 7), (125000, 32), jnp.float32)
        tbl_8 = 0.05 * jax.random.normal(jax.random.fold_in(_tk, 500 + 8), (125000, 32), jnp.float32)
        tbl_9 = 0.05 * jax.random.normal(jax.random.fold_in(_tk, 500 + 9), (12500, 32), jnp.float32)
        tbl_10 = 0.05 * jax.random.normal(jax.random.fold_in(_tk, 500 + 10), (1000, 32), jnp.float32)
        tbl_11 = 0.05 * jax.random.normal(jax.random.fold_in(_tk, 500 + 11), (1000, 32), jnp.float32)
        tbl_12 = 0.05 * jax.random.normal(jax.random.fold_in(_tk, 500 + 12), (1000, 32), jnp.float32)
        tbl_13 = 0.05 * jax.random.normal(jax.random.fold_in(_tk, 500 + 13), (1000, 32), jnp.float32)
        tbl_14 = 0.05 * jax.random.normal(jax.random.fold_in(_tk, 500 + 14), (1000, 32), jnp.float32)
        tbl_15 = 0.05 * jax.random.normal(jax.random.fold_in(_tk, 500 + 15), (1250, 32), jnp.float32)
        tbl_16 = 0.05 * jax.random.normal(jax.random.fold_in(_tk, 500 + 16), (125000, 32), jnp.float32)
        tbl_17 = 0.05 * jax.random.normal(jax.random.fold_in(_tk, 500 + 17), (1250, 32), jnp.float32)
        tbl_18 = 0.05 * jax.random.normal(jax.random.fold_in(_tk, 500 + 18), (1000, 32), jnp.float32)
        tbl_19 = 0.05 * jax.random.normal(jax.random.fold_in(_tk, 500 + 19), (125000, 32), jnp.float32)
        tbl_20 = 0.05 * jax.random.normal(jax.random.fold_in(_tk, 500 + 20), (125000, 32), jnp.float32)
        tbl_21 = 0.05 * jax.random.normal(jax.random.fold_in(_tk, 500 + 21), (125000, 32), jnp.float32)
        tbl_22 = 0.05 * jax.random.normal(jax.random.fold_in(_tk, 500 + 22), (1000, 32), jnp.float32)
        tbl_23 = 0.05 * jax.random.normal(jax.random.fold_in(_tk, 500 + 23), (1250, 32), jnp.float32)
        tbl_24 = 0.05 * jax.random.normal(jax.random.fold_in(_tk, 500 + 24), (1250, 32), jnp.float32)
        tbl_25 = 0.05 * jax.random.normal(jax.random.fold_in(_tk, 500 + 25), (12500, 32), jnp.float32)
        tbl_26 = 0.05 * jax.random.normal(jax.random.fold_in(_tk, 500 + 26), (1250, 32), jnp.float32)
        tbl_27 = 0.05 * jax.random.normal(jax.random.fold_in(_tk, 500 + 27), (1250, 32), jnp.float32)
        tbl_28 = 0.05 * jax.random.normal(jax.random.fold_in(_tk, 500 + 28), (1000, 32), jnp.float32)
        tbl_29 = 0.05 * jax.random.normal(jax.random.fold_in(_tk, 500 + 29), (1000, 32), jnp.float32)
        tbl_30 = 0.05 * jax.random.normal(jax.random.fold_in(_tk, 500 + 30), (1000, 32), jnp.float32)
        tbl_31 = 0.05 * jax.random.normal(jax.random.fold_in(_tk, 500 + 31), (1250, 32), jnp.float32)
        _rk = jax.random.fold_in(_tk, 7)
        W_top1 = 0.0830455 * jax.random.normal(jax.random.fold_in(_tk, 801), (145, 512), jnp.float32)
        W_top2 = 0.0441942 * jax.random.normal(jax.random.fold_in(_tk, 802), (512, 256), jnp.float32)
        W_top3 = 0.0625 * jax.random.normal(jax.random.fold_in(_tk, 803), (256, 1), jnp.float32)
        b_top1 = jnp.zeros((512,), jnp.float32)
        b_top2 = jnp.zeros((256,), jnp.float32)
        return (dense_ctx, ids, tbl_0, tbl_1, tbl_2, tbl_3, tbl_4, tbl_5, tbl_6, tbl_7, tbl_8, tbl_9, tbl_10, tbl_11, tbl_12, tbl_13, tbl_14, tbl_15, tbl_16, tbl_17, tbl_18, tbl_19, tbl_20, tbl_21, tbl_22, tbl_23, tbl_24, tbl_25, tbl_26, tbl_27, tbl_28, tbl_29, tbl_30, tbl_31, W_top1, b_top1, W_top2, b_top2, W_top3)
    dense_ctx, ids, tbl_0, tbl_1, tbl_2, tbl_3, tbl_4, tbl_5, tbl_6, tbl_7, tbl_8, tbl_9, tbl_10, tbl_11, tbl_12, tbl_13, tbl_14, tbl_15, tbl_16, tbl_17, tbl_18, tbl_19, tbl_20, tbl_21, tbl_22, tbl_23, tbl_24, tbl_25, tbl_26, tbl_27, tbl_28, tbl_29, tbl_30, tbl_31, W_top1, b_top1, W_top2, b_top2, W_top3 = _rec_inputs()

    def _L0_rec_setup():
        import jax, jax.numpy as jnp
        import numpy as np

        def _cin(x, Ws, bs):
            B, F, D = x.shape
            h = x
            directs = []
            n_layers = len(Ws)
            for i, (W, b) in enumerate(zip(Ws, bs)):
                O = W.shape[0]
                H = h.shape[1]
                z = jnp.einsum('bhd,bmd,ohm->bod', h, x, W.reshape(O, H, F))
                z = jax.nn.relu(z + b[None, :, None])
                if i < n_layers - 1:
                    half = O // 2
                    h, direct = (z[:, :half, :], z[:, half:, :])
                else:
                    direct = z
                directs.append(direct)
            out = jnp.concatenate(directs, axis=1)
            return jnp.sum(out, axis=-1)
        key = jax.random.key(seed)
        ks = jax.random.split(key, 4)
        B, F, D = (256, 32, 32)
        x = jax.random.normal(ks[0], (B, F, D), dtype=jnp.float32)
        W0 = jax.random.normal(ks[1], (128, 32 * F), dtype=jnp.float32) * 0.05
        W1 = jax.random.normal(ks[2], (128, 64 * F), dtype=jnp.float32) * 0.05
        W2 = jax.random.normal(ks[3], (1, 64 * F), dtype=jnp.float32) * 0.05
        return {'x': x, 'W0': W0, 'b0': jnp.zeros((128,), jnp.float32), 'W1': W1, 'b1': jnp.zeros((128,), jnp.float32), 'W2': W2, 'b2': jnp.zeros((1,), jnp.float32)}
    _L0_rec_all = _L0_rec_setup()
    _L0_rec_in = {k: v for k, v in _L0_rec_all.items() if k in ('W0', 'b0', 'W1', 'b1', 'W2', 'b2')}
    del _L0_rec_all
    return {'dense_ctx': dense_ctx, 'ids': ids, 'tbl_0': tbl_0, 'tbl_1': tbl_1, 'tbl_2': tbl_2, 'tbl_3': tbl_3, 'tbl_4': tbl_4, 'tbl_5': tbl_5, 'tbl_6': tbl_6, 'tbl_7': tbl_7, 'tbl_8': tbl_8, 'tbl_9': tbl_9, 'tbl_10': tbl_10, 'tbl_11': tbl_11, 'tbl_12': tbl_12, 'tbl_13': tbl_13, 'tbl_14': tbl_14, 'tbl_15': tbl_15, 'tbl_16': tbl_16, 'tbl_17': tbl_17, 'tbl_18': tbl_18, 'tbl_19': tbl_19, 'tbl_20': tbl_20, 'tbl_21': tbl_21, 'tbl_22': tbl_22, 'tbl_23': tbl_23, 'tbl_24': tbl_24, 'tbl_25': tbl_25, 'tbl_26': tbl_26, 'tbl_27': tbl_27, 'tbl_28': tbl_28, 'tbl_29': tbl_29, 'tbl_30': tbl_30, 'tbl_31': tbl_31, 'W_top1': W_top1, 'b_top1': b_top1, 'W_top2': W_top2, 'b_top2': b_top2, 'W_top3': W_top3, 'L0_rec_W0': _L0_rec_in['W0'], 'L0_rec_b0': _L0_rec_in['b0'], 'L0_rec_W1': _L0_rec_in['W1'], 'L0_rec_b1': _L0_rec_in['b1'], 'L0_rec_W2': _L0_rec_in['W2'], 'L0_rec_b2': _L0_rec_in['b2']}

def reference(dense_ctx, ids, tbl_0, tbl_1, tbl_2, tbl_3, tbl_4, tbl_5, tbl_6, tbl_7, tbl_8, tbl_9, tbl_10, tbl_11, tbl_12, tbl_13, tbl_14, tbl_15, tbl_16, tbl_17, tbl_18, tbl_19, tbl_20, tbl_21, tbl_22, tbl_23, tbl_24, tbl_25, tbl_26, tbl_27, tbl_28, tbl_29, tbl_30, tbl_31, W_top1, b_top1, W_top2, b_top2, W_top3, L0_rec_W0, L0_rec_b0, L0_rec_W1, L0_rec_b1, L0_rec_W2, L0_rec_b2):
    import jax
    import jax.numpy as jnp

    def _L0_rec_ref(x, W0, b0, W1, b1, W2, b2):
        import jax, jax.numpy as jnp
        import numpy as np

        def _cin(x, Ws, bs):
            B, F, D = x.shape
            h = x
            directs = []
            n_layers = len(Ws)
            for i, (W, b) in enumerate(zip(Ws, bs)):
                O = W.shape[0]
                H = h.shape[1]
                z = jnp.einsum('bhd,bmd,ohm->bod', h, x, W.reshape(O, H, F))
                z = jax.nn.relu(z + b[None, :, None])
                if i < n_layers - 1:
                    half = O // 2
                    h, direct = (z[:, :half, :], z[:, half:, :])
                else:
                    direct = z
                directs.append(direct)
            out = jnp.concatenate(directs, axis=1)
            return jnp.sum(out, axis=-1)
        return _cin(x, (W0, W1, W2), (b0, b1, b2))
    e = jnp.stack([tbl_0[ids[:, 0]], tbl_1[ids[:, 1]], tbl_2[ids[:, 2]], tbl_3[ids[:, 3]], tbl_4[ids[:, 4]], tbl_5[ids[:, 5]], tbl_6[ids[:, 6]], tbl_7[ids[:, 7]], tbl_8[ids[:, 8]], tbl_9[ids[:, 9]], tbl_10[ids[:, 10]], tbl_11[ids[:, 11]], tbl_12[ids[:, 12]], tbl_13[ids[:, 13]], tbl_14[ids[:, 14]], tbl_15[ids[:, 15]], tbl_16[ids[:, 16]], tbl_17[ids[:, 17]], tbl_18[ids[:, 18]], tbl_19[ids[:, 19]], tbl_20[ids[:, 20]], tbl_21[ids[:, 21]], tbl_22[ids[:, 22]], tbl_23[ids[:, 23]], tbl_24[ids[:, 24]], tbl_25[ids[:, 25]], tbl_26[ids[:, 26]], tbl_27[ids[:, 27]], tbl_28[ids[:, 28]], tbl_29[ids[:, 29]], tbl_30[ids[:, 30]], tbl_31[ids[:, 31]]], axis=1)
    z = _L0_rec_ref(e, L0_rec_W0, L0_rec_b0, L0_rec_W1, L0_rec_b1, L0_rec_W2, L0_rec_b2)
    z = z.reshape(z.shape[0], -1)
    h = jnp.concatenate([z, dense_ctx], axis=1)
    h = jnp.maximum(h @ W_top1 + b_top1, 0.0)
    h = jnp.maximum(h @ W_top2 + b_top2, 0.0)
    y = h @ W_top3
    return y

_drawn_inputs = setup_inputs


def setup_inputs(seed=0):
    import zlib

    import numpy as np

    out = dict(_drawn_inputs(seed))
    spreads = {'b_top1': (0.0, 2.0),
     'b_top2': (0.0, 0.447),
     'L0_rec_b0': (0.0, 0.1),
     'L0_rec_b1': (0.0, 0.1)}
    factors = {'tbl_0': 8.0,
     'tbl_1': 8.0,
     'tbl_2': 8.0,
     'tbl_3': 8.0,
     'tbl_4': 8.0,
     'tbl_5': 8.0,
     'tbl_6': 8.0,
     'tbl_7': 8.0,
     'tbl_8': 8.0,
     'tbl_9': 8.0,
     'tbl_10': 8.0,
     'tbl_11': 8.0,
     'tbl_12': 8.0,
     'tbl_13': 8.0,
     'tbl_14': 8.0,
     'tbl_15': 8.0,
     'tbl_16': 8.0,
     'tbl_17': 8.0,
     'tbl_18': 8.0,
     'tbl_19': 8.0,
     'tbl_20': 8.0,
     'tbl_21': 8.0,
     'tbl_22': 8.0,
     'tbl_23': 8.0,
     'tbl_24': 8.0,
     'tbl_25': 8.0,
     'tbl_26': 8.0,
     'tbl_27': 8.0,
     'tbl_28': 8.0,
     'tbl_29': 8.0,
     'tbl_30': 8.0,
     'tbl_31': 8.0,
     'L0_rec_W0': 8.0,
     'L0_rec_W1': 3.63,
     'L0_rec_W2': 8.0,
     'dense_ctx': 3.712}
    for name, (base, spread) in spreads.items():
        noise = np.random.default_rng([zlib.crc32(name.encode()), seed]).standard_normal(out[name].shape)
        drawn = base * np.exp(spread * noise) if base else spread * noise
        out[name] = jnp.asarray(drawn.astype(out[name].dtype))
    for name, factor in factors.items():
        out[name] = (out[name] * factor).astype(out[name].dtype)
    return out
```

```python
from contextlib import ExitStack

import concourse.bass as bass
from concourse import mybir

F32 = mybir.dt.float32
I32 = mybir.dt.int32
ALU = mybir.AluOpType
ACT = mybir.ActivationFunctionType
AX_X = mybir.AxisListType.X

P = 128
BANK = 512
BATCH, FIELDS, DIM = 1024, 32, 32
HID = 64
CHUNK = 1024
ROWS = CHUNK // DIM
CHUNKS = BATCH * DIM // CHUNK
QUADS = P // FIELDS
PART = CHUNK // QUADS
GATHERS = PART // DIM
ROLLS = 4
H_ROLL = 16
UNROLL = 4
RING = 8
T0, T1 = ROLLS, ROLLS * ROLLS
DENSE = 16
TOP1, TOP2 = 512, 256
M1, M2 = TOP1 // P, TOP2 // P


def x_shift(quad, b):
    return ROLLS * quad + b


def first0(c):
    return (c - 1) * (T0 + T1) + T0 if not isinstance(c, int) or c > 0 else 0


def first1(c):
    last = isinstance(c, int) and c == CHUNKS - 1
    return c * (T0 + T1) + T0 + (0 if last else T0)


def build_tower(nc, gather_ids, row_base, table, w0, w0_swapped, w1, w2, b0, b1, b2,
                dense_t, wt1a, wt1b, bt1, wt2, bt2, wt3, out):
    with ExitStack() as ctx:
        def sb(name, shape, dt=F32):
            return ctx.enter_context(nc.sbuf_tensor(name, shape, dt))

        def psum(name, cols):
            return ctx.enter_context(nc.psum_tensor(name, [P, cols], F32))

        def sem(name):
            return ctx.enter_context(nc.semaphore(name))

        x_dram = nc.dram_tensor("x_dram", [CHUNKS, 2, FIELDS, CHUNK], F32).ap()

        w0_sb = sb("w0_sb", [P, T0 + QUADS, P])
        w0_swap = sb("w0_swap", [P, T0 + QUADS, P])
        w1_sb = sb("w1_sb", [P, T1, P])
        w2_sb = sb("w2_sb", [P, QUADS, HID])
        b0_sb = sb("b0_sb", [P, 1])
        b1_sb = sb("b1_sb", [P, 1])
        b2_sb = sb("b2_sb", [P, 1])
        half_ones = sb("half_ones", [P, FIELDS])
        wt1a_sb = sb("wt1a_sb", [P, TOP1])
        wt1b_sb = sb("wt1b_sb", [1 + DENSE, TOP1])
        wt2_sb = sb("wt2_sb", [P, M1, TOP2])
        wt3_sb = sb("wt3_sb", [P, M2])
        bt1_sb = sb("bt1_sb", [P, M1])
        bt2_sb = sb("bt2_sb", [P, M2])
        ids_sb = sb("ids_sb", [P, CHUNKS * GATHERS], I32)
        base_sb = sb("base_sb", [P, UNROLL * GATHERS], I32)
        rows_sb = sb("rows_sb", [P, UNROLL * GATHERS], I32)

        gathered = sb("gathered", [P, UNROLL, PART])
        x_part = sb("x_part", [P, 2, PART])
        x_part16 = sb("x_part16", [P, 2, PART])
        x_base = sb("x_base", [P, 2, CHUNK])
        x_roll = sb("x_roll", [P, 2, ROLLS, CHUNK])
        h_roll = sb("h_roll", [P, 2, ROLLS, CHUNK])
        pairs16 = sb("pairs16", [P, 2, PART])
        prod = sb("prod", [P, RING, CHUNK])
        direct = sb("direct", [P, 2, CHUNK])
        h2 = sb("h2", [P, 2, BANK])
        h2v = sb("h2v", [P, UNROLL, BANK])
        z2_sb = sb("z2_sb", [P, BANK])
        z2_sum = sb("z2_sum", [P, CHUNKS // UNROLL * (BANK // DIM)])
        top_a = sb("top_a", [P, BATCH])
        top_b = sb("top_b", [1 + DENSE, BATCH])
        mlp1 = h_roll[:, 0, :, :]
        mlp2 = x_roll[:, 0, 0:M2, :]
        y_sb = sb("y_sb", [1, BATCH])

        z0_ps = psum("z0_ps", CHUNK)
        z1_ps = psum("z1_ps", CHUNK)
        v_ps = psum("v_ps", BANK)
        z2_ps = psum("z2_ps", BANK)
        mlp_ps = psum("mlp_ps", 2 * BANK)

        ids_loaded = sem("ids_loaded")
        rows_made = sem("rows_made")
        gather_done = [sem(f"gather_done{u}") for u in range(UNROLL)]
        x_stored = [sem(f"x_stored{s}") for s in range(2)]
        x_base_loaded = [sem(f"x_base_loaded{s}") for s in range(2)]
        x_roll_loaded = [[sem(f"x_roll_loaded{s}_{b}") for b in range(ROLLS)] for s in range(2)]
        w0_loaded = sem("w0_loaded")
        w1_loaded = sem("w1_loaded")
        biases_loaded = sem("biases_loaded")
        mlp_loaded = sem("mlp_loaded")
        w0_ready = sem("w0_ready")
        ones_zeroed = sem("ones_zeroed")
        ones_ready = sem("ones_ready")
        pairs16_ready = sem("pairs16_ready")
        prod_ready = sem("prod_ready")
        prod_used = sem("prod_used")
        z0_done = sem("z0_done")
        z1_done = sem("z1_done")
        v_done = sem("v_done")
        z2_done = sem("z2_done")
        h1_ready = sem("h1_ready")
        h1_rolled = [sem(f"h1_rolled{s}") for s in range(2)]
        direct0_ready = sem("direct0_ready")
        direct1_ready = sem("direct1_ready")
        h2_ready = sem("h2_ready")
        h2v_ready = sem("h2v_ready")
        direct_summed = sem("direct_summed")
        z2_relu = sem("z2_relu")
        z2_summed = sem("z2_summed")
        z2_row = sem("z2_row")
        mlp_done = sem("mlp_done")
        mlp_relu = sem("mlp_relu")
        y_ready = sem("y_ready")
        y_stored = sem("y_stored")

        def wait(eng, s, value):
            if not isinstance(value, int) or value > 0:
                eng.wait_ge(s, value)

        def settled(eng, value):
            return value if isinstance(value, int) else eng.snap(eng.to_reg(value))

        def over_chunks(eng, step, tail_chunks=0):
            for u in range(UNROLL):
                step(u, u)
            with eng.Fori(1, CHUNKS // UNROLL - 1) as group:
                for u in range(UNROLL):
                    step(group * UNROLL + u, u)
            for u in range(UNROLL):
                step(CHUNKS - UNROLL + u, u)

        def is_last(c):
            return isinstance(c, int) and c == CHUNKS - 1

        block = ctx.enter_context(nc.Block())

        @block.gpsimd
        def _(pool):
            pool.dma_start(ids_sb[:, :], gather_ids).then_inc(ids_loaded, 16)
            pool.dma_start(base_sb[:, :], row_base).then_inc(ids_loaded, 16)
            nc.gpsimd.memset(half_ones[:, :], 0.0).then_inc(ones_zeroed, 1)
            pool.wait_ge(ones_zeroed, 1)
            nc.gpsimd.memset(half_ones[0:HID, 0:1], 1.0).then_inc(ones_ready, 1)
            nc.gpsimd.memset(half_ones[HID:P, 1:2], 1.0).then_inc(ones_ready, 1)
            pool.wait_ge(ids_loaded, 32)
            pool.wait_ge(ones_ready, 2)

            def gather_group(group):
                cols = UNROLL * GATHERS
                made = settled(pool, group + 1)
                for u in range(UNROLL):
                    wait(pool, gather_done[u], 16 * GATHERS * group)
                    if not isinstance(group, int):
                        pool.wait_ge(x_stored[u % 2], 16 * (group * UNROLL + u - UNROLL - u % 2 + 2))
                nc.gpsimd.tensor_tensor(rows_sb[:, :], ids_sb[:, bass.ds(group * cols, cols)], base_sb[:, :],
                                        ALU.add).then_inc(rows_made, 1)
                pool.wait_ge(ids_loaded, 32)
                pool.wait_ge(rows_made, made)
                for u in range(UNROLL):
                    for g in range(GATHERS):
                        col = u * GATHERS + g
                        nc.gpsimd.indirect_dma_start(
                            gathered[:, u, g * DIM:(g + 1) * DIM], None, table,
                            bass.IndirectOffsetOnAxis(ap=rows_sb[:, col:col + 1], axis=0),
                        ).then_inc(gather_done[u], 16)

            gather_group(0)
            with pool.Fori(1, CHUNKS // UNROLL) as group:
                gather_group(group)

        @block.sync
        def _(sp):
            def store_x(c, u):
                at = c * (2 * FIELDS * CHUNK)
                sp.wait_ge(gather_done[u], 16 * GATHERS * ((c - u) // UNROLL + 1) if isinstance(c, int)
                           else (c - u) * (16 * GATHERS // UNROLL) + 16 * GATHERS)
                for copy in range(2):
                    to = bass.AP(x_dram.tensor, at + copy * (FIELDS * CHUNK),
                                 [[PART, QUADS], [CHUNK, FIELDS], [1, PART]])
                    sp.dma_start(to, gathered[:, u, :]).then_inc(x_stored[u % 2], 16)

            def load_x(c, u):
                s = u % 2
                at = c * (2 * FIELDS * CHUNK)
                reuses = not isinstance(c, int) or c > 1
                stored = settled(sp, 16 * (c - s + 2))
                if reuses:
                    before = settled(sp, c - 1)
                    products0_before = settled(sp, first0(c - 2) + T0)
                    products1_before = [settled(sp, first1(c - 2) + ROLLS * (b + 1)) for b in range(ROLLS)]
                sp.wait_ge(x_stored[s], stored)
                if reuses:
                    sp.wait_ge(v_done, before)
                    sp.wait_ge(pairs16_ready, before)
                    sp.wait_ge(prod_ready, products0_before)
                sp.dma_start(x_base[:, s, :], bass.AP(x_dram.tensor, at, [[0, QUADS], [CHUNK, FIELDS], [1, CHUNK]])
                             ).then_inc(x_base_loaded[s], 16)
                sp.dma_start(x_part[:, s, :], bass.AP(x_dram.tensor, at,
                                                      [[PART, QUADS], [CHUNK, FIELDS], [1, PART]])
                             ).then_inc(x_base_loaded[s], 16)
                sp.dma_start(x_part16[:, s, :], bass.AP(x_dram.tensor, at + FIELDS // 2 * CHUNK,
                                                        [[PART, QUADS], [CHUNK, FIELDS], [1, PART]])
                             ).then_inc(x_base_loaded[s], 16)
                for b in range(ROLLS):
                    if reuses:
                        sp.wait_ge(prod_ready, products1_before[b])
                    src = bass.AP(x_dram.tensor, at + x_shift(0, b) * CHUNK,
                                  [[x_shift(1, 0) * CHUNK, QUADS], [CHUNK, FIELDS], [1, CHUNK]])
                    sp.dma_start(x_roll[:, s, b, :], src).then_inc(x_roll_loaded[s][b], 16)

            store_x(0, 0)

            def step(c, u):
                if not is_last(c):
                    store_x(c + 1, (u + 1) % UNROLL)
                load_x(c, u)

            over_chunks(sp, step)

        @block.vector
        def _(dve):
            dve.wait_ge(w0_loaded, 32)
            nc.vector.tensor_tensor(w0_sb[:, :, :], w0_sb[:, :, :], w0_swap[:, :, :], ALU.add).then_inc(w0_ready, 1)

            def product(n, slot, in0, in1):
                wait(dve, prod_used, n - RING + 1)
                nc.vector.tensor_tensor(prod[:, slot, :], in0, in1, ALU.mult).then_inc(prod_ready, 1)

            def products0(c, u):
                s = u % 2
                slot = 0 if isinstance(c, int) and c == 0 else (first0(u) if u else first0(UNROLL)) % RING
                dve.wait_ge(x_base_loaded[s], (c - s + 2) * 24)
                wait(dve, z0_done, c - 1)
                nc.vector.tensor_tensor(pairs16[:, s, :], x_part[:, s, :], x_part16[:, s, :], ALU.mult
                                        ).then_inc(pairs16_ready, 1)
                for b in range(ROLLS):
                    dve.wait_ge(x_roll_loaded[s][b], (c - s + 2) * 8)
                    product(first0(c) + b, (slot + b) % RING, x_base[:, s, :], x_roll[:, s, b, :])

            def layer2(c, u):
                dve.wait_ge(v_done, c + 1)
                dve.wait_ge(h2_ready, 2 * (c + 1))
                if not isinstance(c, int) or c >= UNROLL:
                    dve.wait_ge(z2_done, z2_group(c, u))
                nc.vector.tensor_tensor(h2v[:, u, :], v_ps[:, :], h2[:, u % 2, :], ALU.mult).then_inc(h2v_ready, 1)

            def sum_direct(c, u):
                dve.wait_ge(direct0_ready, c + 1)
                dve.wait_ge(direct1_ready, c + 1)
                nc.vector.tensor_reduce(top_a[:, bass.ds(c * ROWS, ROWS)],
                                        direct[:, u % 2, :].rearrange("p (r d) -> p r d", d=DIM),
                                        AX_X, ALU.add).then_inc(direct_summed, 1)

            def z2_group(c, u):
                return (c - u) // UNROLL if isinstance(c, int) else group_of[0]

            def sum_z2(group):
                dve.wait_ge(z2_relu, group + 1)
                cols = BANK // DIM
                nc.vector.tensor_reduce(z2_sum[:, bass.ds(group * cols, cols)],
                                        z2_sb[:, :].rearrange("p (r d) -> p r d", d=DIM),
                                        AX_X, ALU.add).then_inc(z2_summed, 1)

            def products1(c, u):
                s = u % 2
                slot = (first1(u) + (T0 if is_last(c) else 0)) % RING
                if is_last(c):
                    slot = first1(c) % RING
                dve.wait_ge(h1_ready, 2 * (c + 1))
                dve.wait_ge(h1_rolled[s], (c - s + 2) * (16 * (ROLLS - 1)))
                for b in range(ROLLS):
                    for a in range(ROLLS):
                        i = b * ROLLS + a
                        product(first1(c) + i, (slot + i) % RING, h_roll[:, s, a, :], x_roll[:, s, b, :])
                        if i == 6 and (not isinstance(c, int) or c > 0):
                            layer2(c - 1, (u - 1) % UNROLL)
                            sum_direct(c - 1, (u - 1) % UNROLL)
                        if i == T1 - 1 and u == 1 and (not isinstance(c, int) or c > UNROLL):
                            sum_z2(z2_group(c, u) - 1)

            group_of = [None]

            def step(c, u):
                if not is_last(c):
                    products0(c + 1, (u + 1) % UNROLL)
                products1(c, u)

            products0(0, 0)
            for u in range(UNROLL):
                step(u, u)
            with dve.Fori(1, CHUNKS // UNROLL - 1) as group:
                for u in range(UNROLL):
                    group_of[0] = group - 1 if u == 0 else group
                    c = group * UNROLL + u
                    if u == 1:
                        step_group = group
                    step(c, u)
            for u in range(UNROLL):
                step(CHUNKS - UNROLL + u, u)
            layer2(CHUNKS - 1, UNROLL - 1)
            sum_direct(CHUNKS - 1, UNROLL - 1)
            sum_z2(CHUNKS // UNROLL - 1)

        @block.tensor
        def _(pe):
            def mm(*args, **kw):
                return nc.tensor.matmul(*args, **kw)

            def accumulate(ps, n, slot, weights, start, stop):
                pe.wait_ge(prod_ready, n + 1)
                for j in range(CHUNK // BANK):
                    cols = slice(j * BANK, (j + 1) * BANK)
                    last = mm(ps[:, cols], weights, prod[:, slot, cols], start=start, stop=stop)
                last.then_inc(prod_used, 1)
                return last

            def layer0(c, u):
                s = u % 2
                slot = 0 if isinstance(c, int) and c == 0 else (first0(u) if u else first0(UNROLL)) % RING
                wait(pe, h1_ready, 2 * c)
                wait(pe, direct0_ready, c)
                accumulate(z0_ps, first0(c), slot, w0_sb[:, 0, :], True, False)
                pe.wait_ge(pairs16_ready, c + 1)
                for q in range(QUADS):
                    mm(z0_ps[:, q * PART:(q + 1) * PART], w0_sb[:, T0 + q, :], pairs16[:, s, :],
                       start=False, stop=False)
                for b in range(1, ROLLS):
                    accumulate(z0_ps, first0(c) + b, (slot + b) % RING, w0_sb[:, b, :], False, b == ROLLS - 1)
                pe.drain().then_inc(z0_done, 1)

            def layer2_v(c, u):
                wait(pe, h2v_ready, c)
                for q in range(QUADS):
                    half, at = divmod(q * PART, BANK)
                    last = mm(v_ps[half * HID:(half + 1) * HID, at:at + PART], w2_sb[:, q, :],
                              x_part[:, u % 2, :], start=True, stop=True)
                last.then_inc(v_done, 1)

            def layer2_sum(h2v_count, z2_relu_count):
                pe.wait_ge(h2v_ready, h2v_count)
                wait(pe, z2_relu, z2_relu_count)
                for u in range(UNROLL):
                    last = mm(z2_ps[FIELDS * u:FIELDS * (u + 1), :], half_ones[:, :], h2v[:, u, :],
                              start=True, stop=True)
                last.then_inc(z2_done, 1)

            def layer1(c, u, group):
                slot = first1(c) % RING if is_last(c) else first1(u) % RING
                wait(pe, h2_ready, 2 * c)
                wait(pe, direct1_ready, c)
                for i in range(T1):
                    last = accumulate(z1_ps, first1(c) + i, (slot + i) % RING, w1_sb[:, i, :], i == 0, i == T1 - 1)
                    if i == 4:
                        layer2_v(c, u)
                    if i == 11 and u == 0 and (not isinstance(c, int) or c > 0):
                        layer2_sum(c, group - 1)
                pe.drain().then_inc(z1_done, 1)

            def step(c, u, group):
                if not is_last(c):
                    layer0(c + 1, (u + 1) % UNROLL)
                layer1(c, u, group)

            pe.wait_ge(w0_ready, 1)
            layer0(0, 0)
            pe.wait_ge(w1_loaded, 32)
            pe.wait_ge(ones_ready, 2)
            for u in range(UNROLL):
                step(u, u, 0)
            with pe.Fori(1, CHUNKS // UNROLL - 1) as group:
                for u in range(UNROLL):
                    step(group * UNROLL + u, u, group)
            for u in range(UNROLL):
                step(CHUNKS - UNROLL + u, u, CHUNKS // UNROLL - 1)
            layer2_sum(CHUNKS, CHUNKS // UNROLL - 1)

            pe.wait_ge(mlp_loaded, 16 * 7)
            pe.wait_ge(direct_summed, CHUNKS)
            pe.wait_ge(z2_row, 16 * 2 * UNROLL)
            n = 0
            halves = BATCH // BANK
            for j in range(halves):
                for m in range(M1):
                    wait(pe, mlp_relu, n - 1)
                    to = mlp_ps[:, n % 2 * BANK:(n % 2 + 1) * BANK]
                    cols = slice(j * BANK, (j + 1) * BANK)
                    mm(to, wt1a_sb[:, m * P:(m + 1) * P], top_a[:, cols], start=True, stop=False)
                    mm(to, wt1b_sb[:, m * P:(m + 1) * P], top_b[:, cols], start=False, stop=True
                       ).then_inc(mlp_done, 1)
                    n += 1
            for j in range(halves):
                pe.wait_ge(mlp_relu, (j + 1) * M1)
                for m in range(M2):
                    wait(pe, mlp_relu, n - 1)
                    for k in range(M1):
                        last = mm(mlp_ps[:, n % 2 * BANK:(n % 2 + 1) * BANK], wt2_sb[:, k, m * P:(m + 1) * P],
                                  mlp1[:, k, j * BANK:(j + 1) * BANK], start=k == 0, stop=k == M1 - 1)
                    last.then_inc(mlp_done, 1)
                    n += 1
            for j in range(halves):
                pe.wait_ge(mlp_relu, halves * M1 + (j + 1) * M2)
                wait(pe, mlp_relu, n - 1)
                for k in range(M2):
                    last = mm(mlp_ps[0:1, n % 2 * BANK:(n % 2 + 1) * BANK], wt3_sb[:, k:k + 1],
                              mlp2[:, k, j * BANK:(j + 1) * BANK], start=k == 0, stop=k == M2 - 1)
                last.then_inc(mlp_done, 1)
                n += 1

        @block.scalar
        def _(act):
            act.dma_start(w0_sb[:, :, :], w0).then_inc(w0_loaded, 16)
            act.dma_start(w0_swap[:, :, :], w0_swapped).then_inc(w0_loaded, 16)
            act.dma_start(b0_sb[:, :], b0).then_inc(biases_loaded, 16)
            act.dma_start(b1_sb[:, :], b1).then_inc(biases_loaded, 16)
            act.dma_start(b2_sb[:, :], b2).then_inc(biases_loaded, 16)
            act.dma_start(w1_sb[:, :, :], w1).then_inc(w1_loaded, 16)
            act.dma_start(w2_sb[:, :, :], w2).then_inc(w1_loaded, 16)
            act.dma_start(wt1a_sb[:, :], wt1a).then_inc(mlp_loaded, 16)
            act.dma_start(wt1b_sb[:, :], wt1b).then_inc(mlp_loaded, 16)
            act.dma_start(wt2_sb[:, :, :], wt2).then_inc(mlp_loaded, 16)
            act.dma_start(wt3_sb[:, :], wt3).then_inc(mlp_loaded, 16)
            act.dma_start(bt1_sb[:, :], bt1).then_inc(mlp_loaded, 16)
            act.dma_start(bt2_sb[:, :], bt2).then_inc(mlp_loaded, 16)
            act.dma_start(top_b[1:1 + DENSE, :], dense_t).then_inc(mlp_loaded, 16)

            def relu0(c, u):
                s = u % 2
                act.wait_ge(z0_done, c + 1)
                if not isinstance(c, int) or c > 1:
                    act.wait_ge(prod_ready, first1(c - 2) + T1)
                for half in range(2):
                    nc.scalar.activation(h_roll[half * HID:(half + 1) * HID, s, 0, :], z0_ps[0:HID, :], ACT.Relu,
                                         bias=b0_sb[0:HID, :]).then_inc(h1_ready, 1)
                wait(act, direct_summed, c - 1)
                nc.scalar.activation(direct[0:HID, s, :], z0_ps[HID:P, :], ACT.Relu,
                                     bias=b0_sb[HID:P, :]).then_inc(direct0_ready, 1)
                act.wait_ge(h1_ready, 2 * (c + 1))
                for a in range(1, ROLLS):
                    r = H_ROLL * a
                    act.dma_start(h_roll[0:P - r, s, a, :], h_roll[r:P, s, 0, :]).then_inc(h1_rolled[s], 16)
                    act.dma_start(h_roll[P - r:P, s, a, :], h_roll[0:r, s, 0, :]).then_inc(h1_rolled[s], 16)

            def relu1(c, u):
                s = u % 2
                act.wait_ge(z1_done, c + 1)
                wait(act, h2v_ready, c - 1)
                for half in range(2):
                    nc.scalar.activation(h2[half * HID:(half + 1) * HID, s, :],
                                         z1_ps[0:HID, half * BANK:(half + 1) * BANK], ACT.Relu,
                                         bias=b1_sb[0:HID, :]).then_inc(h2_ready, 1)
                nc.scalar.activation(direct[HID:P, s, :], z1_ps[HID:P, :], ACT.Relu,
                                     bias=b1_sb[HID:P, :]).then_inc(direct1_ready, 1)

            def relu2(done, summed):
                act.wait_ge(z2_done, done)
                wait(act, z2_summed, summed)
                nc.scalar.activation(z2_sb[:, :], z2_ps[:, :], ACT.Relu, bias=b2_sb[:, :]).then_inc(z2_relu, 1)

            def step(c, u, group):
                if not is_last(c):
                    relu0(c + 1, (u + 1) % UNROLL)
                if u == 0 and (not isinstance(c, int) or c > 0):
                    relu2(group, group - 1)
                relu1(c, u)

            act.wait_ge(biases_loaded, 48)
            relu0(0, 0)
            for u in range(UNROLL):
                step(u, u, 0)
            with act.Fori(1, CHUNKS // UNROLL - 1) as group:
                for u in range(UNROLL):
                    step(group * UNROLL + u, u, group)
            for u in range(UNROLL):
                step(CHUNKS - UNROLL + u, u, CHUNKS // UNROLL - 1)
            relu2(CHUNKS // UNROLL, CHUNKS // UNROLL - 1)

            act.wait_ge(z2_summed, CHUNKS // UNROLL)
            row = top_b[0:1, :].rearrange("p (g u h r) -> p u h g r", u=UNROLL, h=2, r=BANK // DIM)
            for u in range(UNROLL):
                for half in range(2):
                    p = FIELDS * u + half
                    act.dma_start(row[:, u, half, :, :],
                                  z2_sum[p:p + 1, :].rearrange("p (g r) -> p g r", r=BANK // DIM)
                                  ).then_inc(z2_row, 16)

            act.wait_ge(mlp_loaded, 16 * 7)
            act.wait_ge(prod_ready, first1(CHUNKS - 1) + T1)
            n = 0
            halves = BATCH // BANK
            for j in range(halves):
                for m in range(M1):
                    act.wait_ge(mlp_done, n + 1)
                    nc.scalar.activation(mlp1[:, m, j * BANK:(j + 1) * BANK],
                                         mlp_ps[:, n % 2 * BANK:(n % 2 + 1) * BANK], ACT.Relu,
                                         bias=bt1_sb[:, m:m + 1]).then_inc(mlp_relu, 1)
                    n += 1
            for j in range(halves):
                for m in range(M2):
                    act.wait_ge(mlp_done, n + 1)
                    nc.scalar.activation(mlp2[:, m, j * BANK:(j + 1) * BANK],
                                         mlp_ps[:, n % 2 * BANK:(n % 2 + 1) * BANK], ACT.Relu,
                                         bias=bt2_sb[:, m:m + 1]).then_inc(mlp_relu, 1)
                    n += 1
            for j in range(halves):
                act.wait_ge(mlp_done, n + 1)
                nc.scalar.copy(y_sb[:, j * BANK:(j + 1) * BANK],
                               mlp_ps[0:1, n % 2 * BANK:(n % 2 + 1) * BANK]).then_inc(y_ready, 1)
                n += 1
            act.wait_ge(y_ready, halves)
            act.dma_start(out.rearrange("b o -> o b"), y_sb[:, :]).then_inc(y_stored, 16)
            act.wait_ge(y_stored, 16)


def lay_out(inputs):
    import numpy as np
    a = {k: np.asarray(v) for k, v in inputs.items()}
    tables = [a[f"tbl_{f}"] for f in range(FIELDS)]
    first_row = np.cumsum([0] + [t.shape[0] for t in tables[:-1]]).astype(np.int32)
    r = np.arange(P)
    quad, i = r // FIELDS, r % FIELDS

    arrays = {"table": np.concatenate(tables, axis=0)}
    arrays["gather_ids"] = a["ids"].reshape(CHUNKS, QUADS, GATHERS, FIELDS).transpose(1, 3, 0, 2).reshape(P, -1)
    arrays["row_base"] = np.repeat(first_row[i][:, None], UNROLL * GATHERS, axis=1)

    w0 = a["L0_rec_W0"].reshape(P, FIELDS, FIELDS)
    w0_tiles = np.zeros((P, T0 + QUADS, P), w0.dtype)
    w0_swapped = np.zeros_like(w0_tiles)
    for b in range(ROLLS):
        j = (i + x_shift(quad, b)) % FIELDS
        w0_tiles[:, b, :] = w0[:, i, j].T
        keep = r[i != j]
        w0_swapped[keep, b, :] = w0[:, j[keep], i[keep]].T
    low = np.arange(FIELDS // 2)
    for q in range(QUADS):
        w0_tiles[q * FIELDS + low, T0 + q, :] = w0[:, low, low + FIELDS // 2].T
        w0_swapped[q * FIELDS + low, T0 + q, :] = w0[:, low + FIELDS // 2, low].T
    arrays["w0"], arrays["w0_swapped"] = w0_tiles, w0_swapped

    w1 = a["L0_rec_W1"].reshape(P, HID, FIELDS)
    arrays["w1"] = np.stack([w1[:, (r + H_ROLL * k) % HID, (i + x_shift(quad, b)) % FIELDS].T
                             for b in range(ROLLS) for k in range(ROLLS)], axis=1)
    w2 = a["L0_rec_W2"].reshape(HID, FIELDS)
    w2_tiles = np.zeros((P, QUADS, HID), w2.dtype)
    for q in range(QUADS):
        w2_tiles[q * FIELDS:(q + 1) * FIELDS, q, :] = w2.T
    arrays["w2"] = w2_tiles
    arrays["b0"], arrays["b1"] = a["L0_rec_b0"][:, None], a["L0_rec_b1"][:, None]
    arrays["b2"] = np.repeat(a["L0_rec_b2"][:, None], P, axis=0)
    arrays["dense_t"] = a["dense_ctx"].T
    arrays["wt1a"], arrays["wt1b"] = a["W_top1"][:P], a["W_top1"][P:]
    arrays["bt1"] = a["b_top1"].reshape(M1, P).T
    arrays["wt2"] = a["W_top2"].reshape(M1, P, TOP2).transpose(1, 0, 2)
    arrays["bt2"] = a["b_top2"].reshape(M2, P).T
    arrays["wt3"] = a["W_top3"].reshape(M2, P).T
    return {k: np.ascontiguousarray(v) for k, v in arrays.items()}


_ORDER = ["gather_ids", "row_base", "table", "w0", "w0_swapped", "w1", "w2", "b0", "b1", "b2",
          "dense_t", "wt1a", "wt1b", "bt1", "wt2", "bt2", "wt3"]


def kernel(**inputs):
    import numpy as _np
    import concourse.bacc as _bacc
    from concourse import mybir as _mybir
    from concourse.bass_utils import run_bass_kernel_spmd as _run

    nc = _bacc.Bacc("TRN2", target_bir_lowering=False, num_devices=1)
    laid = lay_out(inputs)
    arrays, args = {}, []
    for name in _ORDER:
        arrays[f"in_{name}"] = laid[name]
        args.append(nc.dram_tensor(f"in_{name}", laid[name].shape, _mybir.dt.from_np(laid[name].dtype),
                                   kind="ExternalInput").ap())
    out = nc.dram_tensor("out_y", (BATCH, 1), _mybir.dt.from_np(_np.dtype("float32")), kind="ExternalOutput").ap()
    build_tower(nc, *args, out)
    r = _run(nc, [arrays], core_ids=[0])
    return r.results[0]["out_y"]
```

```python
from contextlib import ExitStack

import concourse.bass as bass
from concourse import mybir

F32 = mybir.dt.float32
F32R = mybir.dt.float32r
I32 = mybir.dt.int32
ALU = mybir.AluOpType
ACT = mybir.ActivationFunctionType
AX_X = mybir.AxisListType.X

P = 128
BANK = 512
BATCH, FIELDS, DIM = 1024, 32, 32
HID = 64
CHUNK = 1024
ROWS = CHUNK // DIM
CHUNKS = BATCH * DIM // CHUNK
QUADS = P // FIELDS
PART = CHUNK // QUADS
GATHERS = PART // DIM
ROLLS = 4
H_ROLL = 16
UNROLL = 4
PAIR = 2
PAIRS0 = ROLLS // PAIR
PAIRS1 = ROLLS
RING = 3
SPLIT_RING = 2
DENSE = 16
TOP1, TOP2 = 512, 256
M1, M2 = TOP1 // P, TOP2 // P


def x_shift(quad, b):
    return ROLLS * quad + b


def first0(c):
    return (c - 1) * (PAIRS0 + PAIRS1) + PAIRS0 if not isinstance(c, int) or c > 0 else 0


def first1(c):
    return c * (PAIRS0 + PAIRS1) + PAIRS0 + (0 if is_last(c) else PAIRS0)


def slot0(c):
    return first0(c) % RING if isinstance(c, int) else first0(1) % RING


def slot1(c):
    return first1(c) % RING if isinstance(c, int) else first1(1) % RING


def is_last(c):
    return isinstance(c, int) and c == CHUNKS - 1


def not_first(c, n=1):
    return not isinstance(c, int) or c >= n


assert (PAIRS0 + PAIRS1) % RING == 0 and PAIRS1 % SPLIT_RING == 0


def build_tower(nc, gather_ids, row_base, table, w0, w0_swapped, w1_whole, w1_split, w2, b0, b1, b2,
                dense_t, wt1a, wt1b, bt1, wt2, bt2, wt3, out):
    with ExitStack() as ctx:
        def sb(name, shape, dt=F32):
            return ctx.enter_context(nc.sbuf_tensor(name, shape, dt))

        def psum(name, cols):
            return ctx.enter_context(nc.psum_tensor(name, [P, cols], F32))

        def sem(name):
            return ctx.enter_context(nc.semaphore(name))

        x_dram = nc.dram_tensor("x_dram", [CHUNKS, 2, FIELDS, CHUNK], F32).ap()

        w0_sb = sb("w0_sb", [P, ROLLS + QUADS, P])
        w1_sb = sb("w1_sb", [P, PAIRS1 * PAIR, P])
        w1_hi = sb("w1_hi", [P, PAIRS1 * PAIR, P], F32R)
        w1_lo = sb("w1_lo", [P, PAIRS1 * PAIR, P], F32R)
        w2_sb = sb("w2_sb", [P, QUADS, HID])
        b0_sb = sb("b0_sb", [P, 1])
        b1_sb = sb("b1_sb", [P, 1])
        b2_sb = sb("b2_sb", [P, 1])
        half_ones = sb("half_ones", [P, FIELDS])
        wt1a_sb = sb("wt1a_sb", [P, TOP1])
        wt1b_sb = sb("wt1b_sb", [P, TOP1])
        wt2_sb = sb("wt2_sb", [P, M1, TOP2])
        wt3_sb = sb("wt3_sb", [P, M2])
        bt1_sb = sb("bt1_sb", [P, M1])
        bt2_sb = sb("bt2_sb", [P, M2])
        ids_sb = sb("ids_sb", [P, CHUNKS * GATHERS], I32)
        base_sb = sb("base_sb", [P, UNROLL * GATHERS], I32)
        rows_sb = sb("rows_sb", [P, UNROLL * GATHERS], I32)

        gathered = sb("gathered", [P, UNROLL, PART])
        x_part = sb("x_part", [P, 2, PART])
        x_part16 = sb("x_part16", [P, 2, PART])
        x_base = sb("x_base", [P, 2, CHUNK])
        x_roll = sb("x_roll", [P, 2, ROLLS, CHUNK])
        h_roll = sb("h_roll", [P, 2, ROLLS, CHUNK])
        pairs16 = sb("pairs16", [P, 2, PART])
        prod = sb("prod", [P, RING, PAIR, CHUNK])
        raw = sb("raw", [P, PAIR, CHUNK])
        prod_hi = sb("prod_hi", [P, SPLIT_RING, PAIR, CHUNK], F32R)
        prod_lo = sb("prod_lo", [P, SPLIT_RING, PAIR, CHUNK], F32R)
        direct = sb("direct", [P, 2, CHUNK])
        h2 = sb("h2", [P, 2, BANK])
        h2v = sb("h2v", [P, UNROLL, BANK])
        z2_sb = sb("z2_sb", [P, BANK])
        z2_sum = sb("z2_sum", [P, CHUNKS // UNROLL * (BANK // DIM)])
        top_a = sb("top_a", [P, BATCH])
        top_b = sb("top_b", [P, BATCH])
        w0_swap = h2v[:, 0:2, :].rearrange("p a (t n) -> p (a t) n", n=P)
        w1_raw = h2v[:, 2:4, :].rearrange("p a (t n) -> p (a t) n", n=P)
        mlp1 = h_roll[:, 0, :, :]
        mlp2 = x_roll[:, 0, 0:M2, :]
        y_sb = direct[0:1, 0, :]

        z0_ps = psum("z0_ps", CHUNK)
        z1_ps = psum("z1_ps", CHUNK)
        v_ps = psum("v_ps", BANK)
        z2_ps = psum("z2_ps", BANK)
        mlp_ps = psum("mlp_ps", 2 * BANK)
        mlp_banks = [t[:, k * BANK:(k + 1) * BANK] for t in (z0_ps, z1_ps, mlp_ps) for k in range(2)]

        ids_loaded = sem("ids_loaded")
        rows_made = sem("rows_made")
        gather_done = [sem(f"gather_done{u}") for u in range(UNROLL)]
        x_stored = [sem(f"x_stored{s}") for s in range(2)]
        x_base_loaded = [sem(f"x_base_loaded{s}") for s in range(2)]
        x_roll_loaded = [[sem(f"x_roll_loaded{s}_{b}") for b in range(ROLLS)] for s in range(2)]
        w0_loaded = sem("w0_loaded")
        w1_loaded = sem("w1_loaded")
        biases_loaded = sem("biases_loaded")
        mlp_loaded = sem("mlp_loaded")
        w0_ready = sem("w0_ready")
        w1_hi_ready = sem("w1_hi_ready")
        w1_ready = sem("w1_ready")
        ones_zeroed = sem("ones_zeroed")
        ones_ready = sem("ones_ready")
        top_b_zeroed = sem("top_b_zeroed")
        pairs16_ready = sem("pairs16_ready")
        prod_ready = sem("prod_ready")
        prod_used = sem("prod_used")
        raw_ready = sem("raw_ready")
        hi_ready = sem("hi_ready")
        lo_ready = sem("lo_ready")
        split_used = sem("split_used")
        v_done = sem("v_done")
        z2_done = sem("z2_done")
        h1_ready = sem("h1_ready")
        h1_rolled = [sem(f"h1_rolled{s}") for s in range(2)]
        direct0_ready = sem("direct0_ready")
        direct1_ready = sem("direct1_ready")
        h2_ready = sem("h2_ready")
        h2v_ready = sem("h2v_ready")
        direct_summed = sem("direct_summed")
        z2_relu = sem("z2_relu")
        z2_summed = sem("z2_summed")
        z2_row = sem("z2_row")
        mlp_done = sem("mlp_done")
        mlp_relu = sem("mlp_relu")
        y_ready = sem("y_ready")
        y_stored = sem("y_stored")

        def wait(eng, s, value):
            if not isinstance(value, int) or value > 0:
                eng.wait_ge(s, value)

        def settled(eng, value):
            return value if isinstance(value, int) else eng.snap(eng.to_reg(value))

        def over_chunks(eng, step):
            groups = CHUNKS // UNROLL
            for u in range(UNROLL):
                step(u, u, 0)
            with eng.Fori(1, groups - 1) as group:
                for u in range(UNROLL):
                    step(group * UNROLL + u, u, group)
            for u in range(UNROLL):
                step((groups - 1) * UNROLL + u, u, groups - 1)

        def rows_of_z2(eng, half):
            eng.wait_ge(z2_summed, CHUNKS // UNROLL)
            row = top_b[0:1, :].rearrange("p (g u h r) -> p u h g r", u=UNROLL, h=2, r=BANK // DIM)
            for u in range(UNROLL):
                p = FIELDS * u + half
                eng.dma_start(row[:, u, half, :, :], z2_sum[p:p + 1, :].rearrange("p (g r) -> p g r", r=BANK // DIM)
                              ).then_inc(z2_row, 16)

        block = ctx.enter_context(nc.Block())

        @block.gpsimd
        def _(pool):
            nc.gpsimd.memset(half_ones[:, :], 0.0).then_inc(ones_zeroed, 1)
            pool.wait_ge(ones_zeroed, 1)
            nc.gpsimd.memset(half_ones[0:HID, 0:1], 1.0).then_inc(ones_ready, 1)
            nc.gpsimd.memset(half_ones[HID:P, 1:2], 1.0).then_inc(ones_ready, 1)
            pool.wait_ge(ids_loaded, 32)
            pool.wait_ge(ones_ready, 2)

            def gather_group(group):
                cols = UNROLL * GATHERS
                made = settled(pool, group + 1)
                for u in range(UNROLL):
                    wait(pool, gather_done[u], 16 * GATHERS * group)
                    if not isinstance(group, int):
                        pool.wait_ge(x_stored[u % 2], 16 * (group * UNROLL + u - UNROLL - u % 2 + 2))
                nc.gpsimd.tensor_tensor(rows_sb[:, :], ids_sb[:, bass.ds(group * cols, cols)], base_sb[:, :],
                                        ALU.add).then_inc(rows_made, 1)
                pool.wait_ge(ids_loaded, 32)
                pool.wait_ge(rows_made, made)
                for u in range(UNROLL):
                    for g in range(GATHERS):
                        col = u * GATHERS + g
                        nc.gpsimd.indirect_dma_start(
                            gathered[:, u, g * DIM:(g + 1) * DIM], None, table,
                            bass.IndirectOffsetOnAxis(ap=rows_sb[:, col:col + 1], axis=0),
                        ).then_inc(gather_done[u], 16)

            gather_group(0)
            with pool.Fori(1, CHUNKS // UNROLL) as group:
                gather_group(group)

        @block.sync
        def _(sp):
            def store_x(c, u):
                at = c * (2 * FIELDS * CHUNK)
                sp.wait_ge(gather_done[u], 16 * GATHERS * ((c - u) // UNROLL + 1) if isinstance(c, int)
                           else (c - u) * (16 * GATHERS // UNROLL) + 16 * GATHERS)
                for copy in range(2):
                    to = bass.AP(x_dram.tensor, at + copy * (FIELDS * CHUNK),
                                 [[PART, QUADS], [CHUNK, FIELDS], [1, PART]])
                    sp.dma_start(to, gathered[:, u, :]).then_inc(x_stored[u % 2], 16)

            def load_x(c, u):
                s = u % 2
                at = c * (2 * FIELDS * CHUNK)
                reuses = not_first(c, 2)
                stored = settled(sp, 16 * (c - s + 2))
                if reuses:
                    before = settled(sp, c - 1)
                    products0_before = settled(sp, first0(c - 2) + PAIRS0)
                    products1_before = [settled(sp, first1(c - 2) + b + 1) for b in range(ROLLS)]
                sp.wait_ge(x_stored[s], stored)
                if reuses:
                    sp.wait_ge(v_done, before)
                    sp.wait_ge(pairs16_ready, before)
                    sp.wait_ge(prod_ready, products0_before)
                sp.dma_start(x_base[:, s, :], bass.AP(x_dram.tensor, at, [[0, QUADS], [CHUNK, FIELDS], [1, CHUNK]])
                             ).then_inc(x_base_loaded[s], 16)
                sp.dma_start(x_part[:, s, :], bass.AP(x_dram.tensor, at,
                                                      [[PART, QUADS], [CHUNK, FIELDS], [1, PART]])
                             ).then_inc(x_base_loaded[s], 16)
                sp.dma_start(x_part16[:, s, :], bass.AP(x_dram.tensor, at + FIELDS // 2 * CHUNK,
                                                        [[PART, QUADS], [CHUNK, FIELDS], [1, PART]])
                             ).then_inc(x_base_loaded[s], 16)
                for b in range(ROLLS):
                    if reuses:
                        sp.wait_ge(prod_ready, products1_before[b])
                    src = bass.AP(x_dram.tensor, at + x_shift(0, b) * CHUNK,
                                  [[x_shift(1, 0) * CHUNK, QUADS], [CHUNK, FIELDS], [1, CHUNK]])
                    sp.dma_start(x_roll[:, s, b, :], src).then_inc(x_roll_loaded[s][b], 16)

            def step(c, u, group):
                store_x(c, u)
                load_x(c, u)

            sp.dma_start(ids_sb[:, :], gather_ids).then_inc(ids_loaded, 16)
            sp.dma_start(base_sb[:, :], row_base).then_inc(ids_loaded, 16)

            over_chunks(sp, step)
            sp.wait_ge(top_b_zeroed, 1)
            rows_of_z2(sp, 1)

        @block.vector
        def _(dve):
            nc.vector.memset(top_b[:, :], 0.0).then_inc(top_b_zeroed, 1)
            dve.wait_ge(w0_loaded, 32)
            nc.vector.tensor_tensor(w0_sb[:, :, :], w0_sb[:, :, :], w0_swap[:, :, :], ALU.add).then_inc(w0_ready, 1)

            def twice(ap):
                return ap.unsqueeze(1).to_broadcast([P, PAIR, CHUNK])

            def whole(n, slot, in0, in1):
                wait(dve, prod_used, n - RING + 1)
                nc.vector.tensor_tensor(prod[:, slot % RING, :, :], in0, in1, ALU.mult).then_inc(prod_ready, 1)

            def products0(c, u):
                s = u % 2
                dve.wait_ge(x_base_loaded[s], (c - s + 2) * 24)
                if not_first(c, 2):
                    dve.wait_ge(prod_used, first0(c - 2) + PAIRS0)
                nc.vector.tensor_tensor(pairs16[:, s, :], x_part[:, s, :], x_part16[:, s, :], ALU.mult
                                        ).then_inc(pairs16_ready, 1)
                for k in range(PAIRS0):
                    for b in range(k * PAIR, (k + 1) * PAIR):
                        dve.wait_ge(x_roll_loaded[s][b], (c - s + 2) * 8)
                    whole(first0(c) + k, slot0(c) + k, twice(x_base[:, s, :]), x_roll[:, s, k * PAIR:(k + 1) * PAIR, :])

            def split_product(c, s, b):
                wait(dve, lo_ready, c * PAIRS1 + b)
                nc.vector.tensor_tensor(raw[:, :, :], h_roll[:, s, PAIR:2 * PAIR, :], twice(x_roll[:, s, b, :]), ALU.mult
                                        ).then_inc(raw_ready, 1)

            def split_rest(c, b):
                dve.wait_ge(hi_ready, c * PAIRS1 + b + 1)
                nc.vector.tensor_tensor(prod_lo[:, b % SPLIT_RING, :, :], raw[:, :, :], prod_hi[:, b % SPLIT_RING, :, :],
                                        ALU.subtract).then_inc(lo_ready, 1)

            def layer2(c, u, group):
                dve.wait_ge(v_done, c + 1)
                dve.wait_ge(h2_ready, 2 * (c + 1))
                wait(dve, z2_done, group)
                nc.vector.tensor_tensor(h2v[:, u, :], v_ps[:, :], h2[:, u % 2, :], ALU.mult).then_inc(h2v_ready, 1)

            def sum_direct(c, u):
                dve.wait_ge(direct0_ready, c + 1)
                dve.wait_ge(direct1_ready, c + 1)
                nc.vector.tensor_reduce(top_a[:, bass.ds(c * ROWS, ROWS)],
                                        direct[:, u % 2, :].rearrange("p (r d) -> p r d", d=DIM),
                                        AX_X, ALU.add).then_inc(direct_summed, 1)

            def sum_z2(group):
                dve.wait_ge(z2_relu, group + 1)
                cols = BANK // DIM
                nc.vector.tensor_reduce(z2_sum[:, bass.ds(group * cols, cols)],
                                        z2_sb[:, :].rearrange("p (r d) -> p r d", d=DIM),
                                        AX_X, ALU.add).then_inc(z2_summed, 1)

            def step(c, u, group):
                s = u % 2
                if not is_last(c):
                    products0(c + 1, (u + 1) % UNROLL)
                dve.wait_ge(h1_ready, 2 * (c + 1))
                dve.wait_ge(h1_rolled[s], (c - s + 2) * (16 * (ROLLS - 1)))
                for b in range(ROLLS):
                    split_product(c, s, b)
                    whole(first1(c) + b, slot1(c) + b, h_roll[:, s, 0:PAIR, :], twice(x_roll[:, s, b, :]))
                    if b == 1 and not_first(c):
                        layer2(c - 1, (u - 1) % UNROLL, group if u else group - 1)
                        sum_direct(c - 1, (u - 1) % UNROLL)
                    if b == 2 and u == 1 and not_first(c, UNROLL):
                        sum_z2(group - 1)
                    split_rest(c, b)

            products0(0, 0)
            dve.wait_ge(w1_loaded, 48)
            nc.vector.tensor_copy(w1_hi[:, :, :], w1_raw).then_inc(w1_hi_ready, 1)
            dve.wait_ge(w1_hi_ready, 1)
            nc.vector.tensor_tensor(w1_lo[:, :, :], w1_raw, w1_hi[:, :, :], ALU.subtract).then_inc(w1_ready, 1)
            over_chunks(dve, step)
            layer2(CHUNKS - 1, UNROLL - 1, CHUNKS // UNROLL - 1)
            sum_direct(CHUNKS - 1, UNROLL - 1)
            sum_z2(CHUNKS // UNROLL - 1)

        @block.tensor
        def _(pe):
            def mm(*args, **kw):
                return nc.tensor.matmul(*args, **kw)

            def over_banks(ps, weights, tile, start=False, stop=False):
                for j in range(CHUNK // BANK):
                    cols = slice(j * BANK, (j + 1) * BANK)
                    last = mm(ps[:, cols], weights, tile[:, cols], start=start, stop=stop)
                return last

            def whole(ps, n, slot, weights, start=False, stop=False):
                pe.wait_ge(prod_ready, n + 1)
                over_banks(ps, weights[:, 0, :], prod[:, slot % RING, 0, :], start=start)
                return over_banks(ps, weights[:, 1, :], prod[:, slot % RING, 1, :], stop=stop).then_inc(prod_used, 1)

            def split(ps, c, b, stop=False):
                pe.wait_ge(lo_ready, c * PAIRS1 + b + 1)
                slot = b % SPLIT_RING
                for k in range(PAIR):
                    t = b * PAIR + k
                    over_banks(ps, w1_hi[:, t, :], prod_hi[:, slot, k, :])
                    over_banks(ps, w1_hi[:, t, :], prod_lo[:, slot, k, :])
                    last = over_banks(ps, w1_lo[:, t, :], prod_hi[:, slot, k, :], stop=stop and k == PAIR - 1)
                return last.then_inc(split_used, 1)

            def layer0(c, u):
                s = u % 2
                wait(pe, h1_ready, 2 * c)
                wait(pe, direct0_ready, c)
                whole(z0_ps, first0(c), slot0(c), w0_sb[:, 0:PAIR, :], start=True)
                pe.wait_ge(pairs16_ready, c + 1)
                for q in range(QUADS):
                    mm(z0_ps[:, q * PART:(q + 1) * PART], w0_sb[:, ROLLS + q, :], pairs16[:, s, :],
                       start=False, stop=False)
                for k in range(1, PAIRS0):
                    whole(z0_ps, first0(c) + k, slot0(c) + k, w0_sb[:, k * PAIR:(k + 1) * PAIR, :],
                          stop=k == PAIRS0 - 1)

            def layer2_v(c, u):
                wait(pe, h2v_ready, c)
                for q in range(QUADS):
                    half, at = divmod(q * PART, BANK)
                    last = mm(v_ps[half * HID:(half + 1) * HID, at:at + PART], w2_sb[:, q, :],
                              x_part[:, u % 2, :], start=True, stop=True)
                last.then_inc(v_done, 1)

            def layer2_sum(h2v_count, z2_relu_count):
                pe.wait_ge(h2v_ready, h2v_count)
                wait(pe, z2_relu, z2_relu_count)
                for u in range(UNROLL):
                    last = mm(z2_ps[FIELDS * u:FIELDS * (u + 1), :], half_ones[:, :], h2v[:, u, :],
                              start=True, stop=True)
                last.then_inc(z2_done, 1)

            def step(c, u, group):
                if not is_last(c):
                    layer0(c + 1, (u + 1) % UNROLL)
                wait(pe, h2_ready, 2 * c)
                wait(pe, direct1_ready, c)
                for b in range(ROLLS):
                    whole(z1_ps, first1(c) + b, slot1(c) + b, w1_sb[:, b * PAIR:(b + 1) * PAIR, :], start=b == 0)
                    split(z1_ps, c, b, stop=b == ROLLS - 1)
                    if b == 1:
                        layer2_v(c, u)
                    if b == 2 and u == 0 and not_first(c):
                        layer2_sum(c, group - 1)

            pe.wait_ge(w0_ready, 1)
            layer0(0, 0)
            pe.wait_ge(w1_ready, 1)
            pe.wait_ge(ones_ready, 2)
            over_chunks(pe, step)
            layer2_sum(CHUNKS, CHUNKS // UNROLL - 1)

            halves = BATCH // BANK
            banks = len(mlp_banks)

            def free_bank(n):
                wait(pe, mlp_relu, n - banks + 1)
                return mlp_banks[n % banks]

            def top1_a(n):
                j, m = divmod(n, M1)
                mm(free_bank(n), wt1a_sb[:, m * P:(m + 1) * P], top_a[:, j * BANK:(j + 1) * BANK],
                   start=True, stop=False)

            def top1_b(n):
                j, m = divmod(n, M1)
                mm(mlp_banks[n % banks], wt1b_sb[:, m * P:(m + 1) * P], top_b[:, j * BANK:(j + 1) * BANK],
                   start=False, stop=True).then_inc(mlp_done, 1)

            pe.wait_ge(mlp_loaded, 16 * 7)
            pe.wait_ge(direct_summed, CHUNKS)
            pe.wait_ge(h2_ready, 2 * CHUNKS)
            for n in range(banks):
                top1_a(n)
            pe.wait_ge(z2_row, 16 * 2 * UNROLL)
            for n in range(halves * M1):
                if n >= banks:
                    top1_a(n)
                top1_b(n)
            n = halves * M1
            for j in range(halves):
                pe.wait_ge(mlp_relu, (j + 1) * M1)
                for m in range(M2):
                    to = free_bank(n)
                    for k in range(M1):
                        last = mm(to, wt2_sb[:, k, m * P:(m + 1) * P],
                                  mlp1[:, k, j * BANK:(j + 1) * BANK], start=k == 0, stop=k == M1 - 1)
                    last.then_inc(mlp_done, 1)
                    n += 1
            for j in range(halves):
                pe.wait_ge(mlp_relu, halves * M1 + (j + 1) * M2)
                to = free_bank(n)
                for k in range(M2):
                    last = mm(to[0:1, :], wt3_sb[:, k:k + 1],
                              mlp2[:, k, j * BANK:(j + 1) * BANK], start=k == 0, stop=k == M2 - 1)
                last.then_inc(mlp_done, 1)
                n += 1

        @block.scalar
        def _(act):
            act.dma_start(w0_sb[:, :, :], w0).then_inc(w0_loaded, 16)
            act.dma_start(w0_swap[:, :, :], w0_swapped).then_inc(w0_loaded, 16)
            act.dma_start(b0_sb[:, :], b0).then_inc(biases_loaded, 16)
            act.dma_start(b1_sb[:, :], b1).then_inc(biases_loaded, 16)
            act.dma_start(b2_sb[:, :], b2).then_inc(biases_loaded, 16)
            act.dma_start(w1_raw, w1_split).then_inc(w1_loaded, 16)
            act.dma_start(w1_sb[:, :, :], w1_whole).then_inc(w1_loaded, 16)
            act.dma_start(w2_sb[:, :, :], w2).then_inc(w1_loaded, 16)
            act.dma_start(wt1a_sb[:, :], wt1a).then_inc(mlp_loaded, 16)
            act.dma_start(wt1b_sb[:, :], wt1b).then_inc(mlp_loaded, 16)
            act.dma_start(wt2_sb[:, :, :], wt2).then_inc(mlp_loaded, 16)
            act.dma_start(wt3_sb[:, :], wt3).then_inc(mlp_loaded, 16)
            act.dma_start(bt1_sb[:, :], bt1).then_inc(mlp_loaded, 16)
            act.dma_start(bt2_sb[:, :], bt2).then_inc(mlp_loaded, 16)
            act.wait_ge(top_b_zeroed, 1)
            act.dma_start(top_b[1:1 + DENSE, :], dense_t).then_inc(mlp_loaded, 16)

            def relu0(c, u):
                s = u % 2
                act.wait_ge(prod_used, first0(c) + PAIRS0)
                if not_first(c, 2):
                    act.wait_ge(prod_ready, first1(c - 2) + PAIRS1)
                for half in range(2):
                    nc.scalar.activation(h_roll[half * HID:(half + 1) * HID, s, 0, :], z0_ps[0:HID, :], ACT.Relu,
                                         bias=b0_sb[0:HID, :]).then_inc(h1_ready, 1)
                wait(act, direct_summed, c - 1)
                nc.scalar.activation(direct[0:HID, s, :], z0_ps[HID:P, :], ACT.Relu,
                                     bias=b0_sb[HID:P, :]).then_inc(direct0_ready, 1)
                act.wait_ge(h1_ready, 2 * (c + 1))
                for a in range(1, ROLLS):
                    r = H_ROLL * a
                    act.dma_start(h_roll[0:P - r, s, a, :], h_roll[r:P, s, 0, :]).then_inc(h1_rolled[s], 16)
                    act.dma_start(h_roll[P - r:P, s, a, :], h_roll[0:r, s, 0, :]).then_inc(h1_rolled[s], 16)

            def relu1(c, u):
                s = u % 2
                act.wait_ge(split_used, (c + 1) * PAIRS1)
                wait(act, h2v_ready, c - 1)
                for half in range(2):
                    nc.scalar.activation(h2[half * HID:(half + 1) * HID, s, :],
                                         z1_ps[0:HID, half * BANK:(half + 1) * BANK], ACT.Relu,
                                         bias=b1_sb[0:HID, :]).then_inc(h2_ready, 1)
                nc.scalar.activation(direct[HID:P, s, :], z1_ps[HID:P, :], ACT.Relu,
                                     bias=b1_sb[HID:P, :]).then_inc(direct1_ready, 1)

            def relu2(done, summed):
                act.wait_ge(z2_done, done)
                wait(act, z2_summed, summed)
                nc.scalar.activation(z2_sb[:, :], z2_ps[:, :], ACT.Relu, bias=b2_sb[:, :]).then_inc(z2_relu, 1)

            def round_products(c, b):
                act.wait_ge(raw_ready, c * PAIRS1 + b + 1)
                wait(act, split_used, c * PAIRS1 + b + 1 - SPLIT_RING)
                nc.scalar.copy(prod_hi[:, b % SPLIT_RING, :, :], raw[:, :, :]).then_inc(hi_ready, 1)

            def step(c, u, group):
                round_products(c, 0)
                if not_first(c):
                    relu1(c - 1, (u - 1) % UNROLL)
                round_products(c, 1)
                if not is_last(c):
                    relu0(c + 1, (u + 1) % UNROLL)
                round_products(c, 2)
                round_products(c, 3)
                if u == 0 and not_first(c):
                    relu2(group, group - 1)

            act.wait_ge(biases_loaded, 48)
            relu0(0, 0)
            over_chunks(act, step)
            relu1(CHUNKS - 1, UNROLL - 1)
            relu2(CHUNKS // UNROLL, CHUNKS // UNROLL - 1)

            rows_of_z2(act, 0)
            act.wait_ge(mlp_loaded, 16 * 7)
            act.wait_ge(prod_ready, first1(CHUNKS - 1) + PAIRS1)
            n = 0
            halves = BATCH // BANK
            for j in range(halves):
                for m in range(M1):
                    act.wait_ge(mlp_done, n + 1)
                    nc.scalar.activation(mlp1[:, m, j * BANK:(j + 1) * BANK],
                                         mlp_banks[n % len(mlp_banks)], ACT.Relu,
                                         bias=bt1_sb[:, m:m + 1]).then_inc(mlp_relu, 1)
                    n += 1
            for j in range(halves):
                for m in range(M2):
                    act.wait_ge(mlp_done, n + 1)
                    nc.scalar.activation(mlp2[:, m, j * BANK:(j + 1) * BANK],
                                         mlp_banks[n % len(mlp_banks)], ACT.Relu,
                                         bias=bt2_sb[:, m:m + 1]).then_inc(mlp_relu, 1)
                    n += 1
            for j in range(halves):
                act.wait_ge(mlp_done, n + 1)
                nc.scalar.copy(y_sb[:, j * BANK:(j + 1) * BANK],
                               mlp_banks[n % len(mlp_banks)][0:1, :]).then_inc(y_ready, 1)
                n += 1
            act.wait_ge(y_ready, halves)
            act.dma_start(out.rearrange("b o -> o b"), y_sb[:, :]).then_inc(y_stored, 16)
            act.wait_ge(y_stored, 16)


def lay_out(inputs):
    import numpy as np
    a = {k: np.asarray(v) for k, v in inputs.items()}
    tables = [a[f"tbl_{f}"] for f in range(FIELDS)]
    first_row = np.cumsum([0] + [t.shape[0] for t in tables[:-1]]).astype(np.int32)
    r = np.arange(P)
    quad, i = r // FIELDS, r % FIELDS

    arrays = {"table": np.concatenate(tables, axis=0)}
    arrays["gather_ids"] = a["ids"].reshape(CHUNKS, QUADS, GATHERS, FIELDS).transpose(1, 3, 0, 2).reshape(P, -1)
    arrays["row_base"] = np.repeat(first_row[i][:, None], UNROLL * GATHERS, axis=1)

    w0 = a["L0_rec_W0"].reshape(P, FIELDS, FIELDS)
    w0_tiles = np.zeros((P, ROLLS + QUADS, P), w0.dtype)
    w0_swapped = np.zeros_like(w0_tiles)
    for b in range(ROLLS):
        j = (i + x_shift(quad, b)) % FIELDS
        w0_tiles[:, b, :] = w0[:, i, j].T
        keep = r[i != j]
        w0_swapped[keep, b, :] = w0[:, j[keep], i[keep]].T
    low = np.arange(FIELDS // 2)
    for q in range(QUADS):
        w0_tiles[q * FIELDS + low, ROLLS + q, :] = w0[:, low, low + FIELDS // 2].T
        w0_swapped[q * FIELDS + low, ROLLS + q, :] = w0[:, low + FIELDS // 2, low].T
    arrays["w0"], arrays["w0_swapped"] = w0_tiles, w0_swapped

    w1 = a["L0_rec_W1"].reshape(P, HID, FIELDS)
    for name, copies in (("w1_whole", range(0, PAIR)), ("w1_split", range(PAIR, ROLLS))):
        arrays[name] = np.stack([w1[:, (r + H_ROLL * k) % HID, (i + x_shift(quad, b)) % FIELDS].T
                                 for b in range(ROLLS) for k in copies], axis=1)
    w2 = a["L0_rec_W2"].reshape(HID, FIELDS)
    w2_tiles = np.zeros((P, QUADS, HID), w2.dtype)
    for q in range(QUADS):
        w2_tiles[q * FIELDS:(q + 1) * FIELDS, q, :] = w2.T
    arrays["w2"] = w2_tiles
    arrays["b0"], arrays["b1"] = a["L0_rec_b0"][:, None], a["L0_rec_b1"][:, None]
    arrays["b2"] = np.repeat(a["L0_rec_b2"][:, None], P, axis=0)
    arrays["dense_t"] = a["dense_ctx"].T
    arrays["wt1a"] = a["W_top1"][:P]
    arrays["wt1b"] = np.pad(a["W_top1"][P:], ((0, P - 1 - DENSE), (0, 0)))
    arrays["bt1"] = a["b_top1"].reshape(M1, P).T
    arrays["wt2"] = a["W_top2"].reshape(M1, P, TOP2).transpose(1, 0, 2)
    arrays["bt2"] = a["b_top2"].reshape(M2, P).T
    arrays["wt3"] = a["W_top3"].reshape(M2, P).T
    return {k: np.ascontiguousarray(v) for k, v in arrays.items()}


_ORDER = ["gather_ids", "row_base", "table", "w0", "w0_swapped", "w1_whole", "w1_split", "w2", "b0", "b1", "b2",
          "dense_t", "wt1a", "wt1b", "bt1", "wt2", "bt2", "wt3"]


def kernel(**inputs):
    import numpy as _np
    import concourse.bacc as _bacc
    from concourse import mybir as _mybir
    from concourse.bass_utils import run_bass_kernel_spmd as _run

    nc = _bacc.Bacc("TRN2", target_bir_lowering=False, num_devices=1)
    laid = lay_out(inputs)
    arrays, args = {}, []
    for name in _ORDER:
        arrays[f"in_{name}"] = laid[name]
        args.append(nc.dram_tensor(f"in_{name}", laid[name].shape, _mybir.dt.from_np(laid[name].dtype),
                                   kind="ExternalInput").ap())
    out = nc.dram_tensor("out_y", (BATCH, 1), _mybir.dt.from_np(_np.dtype("float32")), kind="ExternalOutput").ap()
    build_tower(nc, *args, out)
    r = _run(nc, [arrays], core_ids=[0])
    return r.results[0]["out_y"]
```

```python
from contextlib import ExitStack

import concourse.bass as bass
from concourse import mybir

F32 = mybir.dt.float32
F32R = mybir.dt.float32r
I32 = mybir.dt.int32
ALU = mybir.AluOpType
ACT = mybir.ActivationFunctionType
AX_X = mybir.AxisListType.X

P = 128
BANK = 512
BATCH, FIELDS, DIM = 1024, 32, 32
HID = 64
CHUNK = 1024
ROWS = CHUNK // DIM
CHUNKS = BATCH * DIM // CHUNK
QUADS = P // FIELDS
PART = CHUNK // QUADS
GATHERS = PART // DIM
ROLLS = 4
H_ROLL = 16
UNROLL = 4
PAIR = 2
PAIRS0 = ROLLS // PAIR
PAIRS1 = ROLLS
RING = 3
SPLIT_RING = 2
DENSE = 16
TOP1, TOP2 = 512, 256
M1, M2 = TOP1 // P, TOP2 // P
BATCH_HALVES = BATCH // BANK


def x_shift(quad, b):
    return ROLLS * quad + b


def first0(c):
    return (c - 1) * (PAIRS0 + PAIRS1) + PAIRS0 if not isinstance(c, int) or c > 0 else 0


def first1(c):
    return c * (PAIRS0 + PAIRS1) + PAIRS0 + (0 if is_last(c) else PAIRS0)


def slot0(c):
    return first0(c) % RING if isinstance(c, int) else first0(1) % RING


def slot1(c):
    return first1(c) % RING if isinstance(c, int) else first1(1) % RING


def is_last(c):
    return isinstance(c, int) and c == CHUNKS - 1


def is_first(c):
    return isinstance(c, int) and c == 0


def not_first(c, n=1):
    return not isinstance(c, int) or c >= n


def y_partition(j):
    return FIELDS * j


assert (PAIRS0 + PAIRS1) % RING == 0 and PAIRS1 % SPLIT_RING == 0


def build_tower(nc, gather_ids, row_base, table, w0, w0_swapped, w1_whole, w1_split, w2, b0, b1, b2,
                dense_t, wt1a, wt1b, bt1, wt2, bt2, wt3, out):
    with ExitStack() as ctx:
        def sb(name, shape, dt=F32):
            return ctx.enter_context(nc.sbuf_tensor(name, shape, dt))

        def psum(name, cols):
            return ctx.enter_context(nc.psum_tensor(name, [P, cols], F32))

        def sem(name):
            return ctx.enter_context(nc.semaphore(name))

        x_dram = nc.dram_tensor("x_dram", [CHUNKS, 2, FIELDS, CHUNK], F32).ap()

        w0_sb = sb("w0_sb", [P, ROLLS, P])
        w16_sb = sb("w16_sb", [P, QUADS, P], F32R)
        w1_sb = sb("w1_sb", [P, PAIRS1 * PAIR, P])
        w1_hi = sb("w1_hi", [P, PAIRS1 * PAIR, P], F32R)
        w1_lo = sb("w1_lo", [P, PAIRS1 * PAIR, P], F32R)
        w2_sb = sb("w2_sb", [P, QUADS, HID])
        b0_sb = sb("b0_sb", [P, 1])
        b1_sb = sb("b1_sb", [P, 1])
        b2_sb = sb("b2_sb", [P, 1])
        half_ones = sb("half_ones", [P, FIELDS])
        wt1a_sb = sb("wt1a_sb", [P, TOP1])
        wt1b_sb = sb("wt1b_sb", [P, TOP1])
        wt2_sb = sb("wt2_sb", [P, M1, TOP2])
        wt3_sb = sb("wt3_sb", [P, M2])
        bt1_sb = sb("bt1_sb", [P, M1])
        bt2_sb = sb("bt2_sb", [P, M2])
        ids_sb = sb("ids_sb", [P, CHUNKS * GATHERS], I32)
        base_sb = sb("base_sb", [P, UNROLL * GATHERS], I32)
        rows_sb = sb("rows_sb", [P, UNROLL * GATHERS], I32)
        table_warm = sb("table_warm", [P, 1])

        gathered = sb("gathered", [P, UNROLL, PART])
        x_part = sb("x_part", [P, 2, PART])
        x_part16 = sb("x_part16", [P, 2, PART])
        x_base = sb("x_base", [P, 2, CHUNK])
        x_roll = sb("x_roll", [P, 2, ROLLS, CHUNK])
        h_roll = sb("h_roll", [P, 2, ROLLS, CHUNK])
        raw16 = sb("raw16", [P, PART])
        hi16 = sb("hi16", [P, PART], F32R)
        lo16 = sb("lo16", [P, PART], F32R)
        prod = sb("prod", [P, RING, PAIR, CHUNK])
        raw = sb("raw", [P, PAIR, CHUNK])
        prod_hi = sb("prod_hi", [P, SPLIT_RING, PAIR, CHUNK], F32R)
        prod_lo = sb("prod_lo", [P, SPLIT_RING, PAIR, CHUNK], F32R)
        direct = sb("direct", [P, 2, CHUNK])
        h2 = sb("h2", [P, 2, BANK])
        h2v = sb("h2v", [P, UNROLL, BANK])
        z2_sb = sb("z2_sb", [P, BANK])
        z2_sum = sb("z2_sum", [P, CHUNKS // UNROLL * (BANK // DIM)])
        top_a = sb("top_a", [P, BATCH])
        top_b = sb("top_b", [P, BATCH])
        w0_swap = h2v[:, 0, :].rearrange("p (t n) -> p t n", n=P)
        w16_raw = h2v[:, 1, :].rearrange("p (t n) -> p t n", n=P)
        w1_raw = h2v[:, 2:4, :].rearrange("p a (t n) -> p (a t) n", n=P)
        w16_swap = z2_sb[:, :].rearrange("p (t n) -> p t n", n=P)
        w16_rest = h2[:, 0, :].rearrange("p (t n) -> p t n", n=P)
        mlp1 = h_roll[:, 0, :, :]
        mlp1_hi = prod_hi[:, :, :, :].rearrange("p s k n -> p (s k) n")
        mlp1_lo = prod_lo[:, :, :, :].rearrange("p s k n -> p (s k) n")
        wt2_hi = w1_hi[:, :, :].rearrange("p t n -> p (t n)").rearrange("p (k n) -> p k n", n=TOP2)
        wt2_lo = w1_lo[:, :, :].rearrange("p t n -> p (t n)").rearrange("p (k n) -> p k n", n=TOP2)
        mlp2 = x_roll[:, 0, 0:M2, :]
        y_sb = direct[:, 0, 0:BANK]

        z0_ps = psum("z0_ps", CHUNK)
        z1_ps = psum("z1_ps", CHUNK)
        v_ps = psum("v_ps", BANK)
        z2_ps = psum("z2_ps", BANK)
        mlp_ps = psum("mlp_ps", 2 * BANK)
        mlp_banks = [t[:, k * BANK:(k + 1) * BANK] for t in (z0_ps, mlp_ps, z1_ps) for k in range(2)]

        ids_loaded = sem("ids_loaded")
        rows_made = sem("rows_made")
        gather_done = [sem(f"gather_done{u}") for u in range(UNROLL)]
        x_stored = [sem(f"x_stored{s}") for s in range(2)]
        x_base_loaded = [sem(f"x_base_loaded{s}") for s in range(2)]
        x_part_loaded = [sem(f"x_part_loaded{s}") for s in range(2)]
        x_roll_loaded = [[sem(f"x_roll_loaded{s}_{b}") for b in range(ROLLS)] for s in range(2)]
        w0_loaded = sem("w0_loaded")
        w1_loaded = sem("w1_loaded")
        biases_loaded = sem("biases_loaded")
        mlp_loaded = sem("mlp_loaded")
        w16_loaded = sem("w16_loaded")
        w0_ready = sem("w0_ready")
        w16_summed = sem("w16_summed")
        w16_hi_ready = sem("w16_hi_ready")
        w16_rest_ready = sem("w16_rest_ready")
        w16_rest_placed = sem("w16_rest_placed")
        w16_ready = sem("w16_ready")
        w1_hi_ready = sem("w1_hi_ready")
        w1_ready = sem("w1_ready")
        ones_zeroed = sem("ones_zeroed")
        ones_ready = sem("ones_ready")
        top_b_zeroed = sem("top_b_zeroed")
        raw16_ready = sem("raw16_ready")
        hi16_ready = sem("hi16_ready")
        lo16_ready = sem("lo16_ready")
        pairs16_used = sem("pairs16_used")
        first_tile_ready = sem("first_tile_ready")
        prod_ready = sem("prod_ready")
        prod_used = sem("prod_used")
        raw_ready = sem("raw_ready")
        hi_ready = sem("hi_ready")
        lo_ready = sem("lo_ready")
        split_used = sem("split_used")
        v_done = sem("v_done")
        z2_done = sem("z2_done")
        h1_ready = sem("h1_ready")
        h1_rolled = [[sem(f"h1_rolled{s}_{a}") for a in range(1, ROLLS)] for s in range(2)]
        direct0_ready = sem("direct0_ready")
        direct1_ready = sem("direct1_ready")
        h2_ready = sem("h2_ready")
        h2v_ready = sem("h2v_ready")
        direct_summed = sem("direct_summed")
        z2_relu = sem("z2_relu")
        z2_summed = sem("z2_summed")
        z2_row = [sem(f"z2_row{j}") for j in range(BATCH_HALVES)]
        mlp_done = sem("mlp_done")
        mlp_relu = sem("mlp_relu")
        mlp1_rounded = sem("mlp1_rounded")
        mlp1_split = sem("mlp1_split")
        wt2_hi_ready = sem("wt2_hi_ready")
        wt2_ready = sem("wt2_ready")
        y_ready = [sem(f"y_ready{j}") for j in range(BATCH_HALVES)]
        y_stored = sem("y_stored")

        def wait(eng, s, value):
            if not isinstance(value, int) or value > 0:
                eng.wait_ge(s, value)

        def settled(eng, value):
            return value if isinstance(value, int) else eng.snap(eng.to_reg(value))

        def over_chunks(eng, step):
            groups = CHUNKS // UNROLL
            for u in range(UNROLL):
                step(u, u, 0)
            with eng.Fori(1, groups - 1) as group:
                for u in range(UNROLL):
                    step(group * UNROLL + u, u, group)
            for u in range(UNROLL):
                step((groups - 1) * UNROLL + u, u, groups - 1)

        def row_of_z2(eng, j, u, h):
            groups = CHUNKS // UNROLL // BATCH_HALVES
            rows = BANK // DIM
            row = top_b[0:1, :].rearrange("p (g u h r) -> p u h g r", u=UNROLL, h=2, r=rows)
            sums = z2_sum[FIELDS * u + h:FIELDS * u + h + 1, :].rearrange("p (g r) -> p g r", r=rows)
            eng.dma_start(row[:, u, h, j * groups:(j + 1) * groups, :], sums[:, j * groups:(j + 1) * groups, :]
                          ).then_inc(z2_row[j], 16)

        block = ctx.enter_context(nc.Block())

        @block.gpsimd
        def _(pool):
            nc.gpsimd.memset(half_ones[:, :], 0.0).then_inc(ones_zeroed, 1)
            pool.wait_ge(ones_zeroed, 1)
            nc.gpsimd.memset(half_ones[0:HID, 0:1], 1.0).then_inc(ones_ready, 1)
            nc.gpsimd.memset(half_ones[HID:P, 1:2], 1.0).then_inc(ones_ready, 1)
            pool.wait_ge(ids_loaded, 32)
            pool.wait_ge(ones_ready, 2)

            def gather_group(group):
                cols = UNROLL * GATHERS
                made = settled(pool, group + 1)
                for u in range(UNROLL):
                    wait(pool, gather_done[u], 16 * GATHERS * group)
                    if not isinstance(group, int):
                        pool.wait_ge(x_stored[u % 2], 16 * (group * UNROLL + u - UNROLL - u % 2 + 2))
                nc.gpsimd.tensor_tensor(rows_sb[:, :], ids_sb[:, bass.ds(group * cols, cols)], base_sb[:, :],
                                        ALU.add).then_inc(rows_made, 1)
                pool.wait_ge(ids_loaded, 32)
                pool.wait_ge(rows_made, made)
                for u in range(UNROLL):
                    for g in range(GATHERS):
                        col = u * GATHERS + g
                        nc.gpsimd.indirect_dma_start(
                            gathered[:, u, g * DIM:(g + 1) * DIM], None, table,
                            bass.IndirectOffsetOnAxis(ap=rows_sb[:, col:col + 1], axis=0),
                        ).then_inc(gather_done[u], 16)

            gather_group(0)
            with pool.Fori(1, CHUNKS // UNROLL) as group:
                gather_group(group)

        @block.sync
        def _(sp):
            def store_x(c, u, group):
                at = c * (2 * FIELDS * CHUNK)
                sp.wait_ge(gather_done[u], (group + 1) * (16 * GATHERS))
                for copy in range(2):
                    to = bass.AP(x_dram.tensor, at + copy * (FIELDS * CHUNK),
                                 [[PART, QUADS], [CHUNK, FIELDS], [1, PART]])
                    sp.dma_start(to, gathered[:, u, :]).then_inc(x_stored[u % 2], 16)

            def load_x(c, u):
                s = u % 2
                at = c * (2 * FIELDS * CHUNK)
                reuses = not_first(c, 2)
                stored = settled(sp, 16 * (c - s + 2))
                if reuses:
                    before = settled(sp, c - 1)
                    products0_before = settled(sp, first0(c - 2) + PAIRS0)
                    products1_before = [settled(sp, first1(c - 2) + b + 1) for b in range(ROLLS)]
                sp.wait_ge(x_stored[s], stored)
                if reuses:
                    sp.wait_ge(prod_ready, products0_before)
                sp.dma_start(x_base[:, s, :], bass.AP(x_dram.tensor, at, [[0, QUADS], [CHUNK, FIELDS], [1, CHUNK]])
                             ).then_inc(x_base_loaded[s], 16)
                for b in range(ROLLS):
                    if reuses:
                        sp.wait_ge(prod_ready, products1_before[b])
                        if b == 0 and is_first(c - 2):
                            sp.wait_ge(raw_ready, 1)
                    src = bass.AP(x_dram.tensor, at + x_shift(0, b) * CHUNK,
                                  [[x_shift(1, 0) * CHUNK, QUADS], [CHUNK, FIELDS], [1, CHUNK]])
                    sp.dma_start(x_roll[:, s, b, :], src).then_inc(x_roll_loaded[s][b], 16)
                if reuses:
                    sp.wait_ge(v_done, before)
                    sp.wait_ge(raw16_ready, before)
                sp.dma_start(x_part[:, s, :], bass.AP(x_dram.tensor, at,
                                                      [[PART, QUADS], [CHUNK, FIELDS], [1, PART]])
                             ).then_inc(x_part_loaded[s], 16)
                sp.dma_start(x_part16[:, s, :], bass.AP(x_dram.tensor, at + FIELDS // 2 * CHUNK,
                                                        [[PART, QUADS], [CHUNK, FIELDS], [1, PART]])
                             ).then_inc(x_part_loaded[s], 16)

            def step(c, u, group):
                store_x(c, u, group)
                load_x(c, u)

            sp.dma_start(ids_sb[:, :], gather_ids).then_inc(ids_loaded, 16)

            over_chunks(sp, step)
            sp.wait_ge(top_b_zeroed, 1)
            for j in range(BATCH_HALVES):
                sp.wait_ge(z2_summed, CHUNKS // UNROLL // BATCH_HALVES * (j + 1))
                for u in range(UNROLL):
                    for h in range(2):
                        if j < BATCH_HALVES - 1 or h == 1:
                            row_of_z2(sp, j, u, h)

        @block.vector
        def _(dve):
            nc.vector.memset(top_b[:, :], 0.0).then_inc(top_b_zeroed, 1)
            dve.wait_ge(w0_loaded, 32)
            nc.vector.tensor_tensor(w0_sb[:, :, :], w0_sb[:, :, :], w0_swap, ALU.add).then_inc(w0_ready, 1)
            dve.wait_ge(w16_loaded, 32)
            nc.vector.tensor_tensor(w16_raw, w16_raw, w16_swap, ALU.add).then_inc(w16_summed, 1)
            dve.wait_ge(w16_summed, 1)
            nc.vector.tensor_copy(w16_sb[:, :, :], w16_raw).then_inc(w16_hi_ready, 1)
            dve.wait_ge(w16_hi_ready, 1)
            nc.vector.tensor_tensor(w16_rest, w16_raw, w16_sb[:, :, :], ALU.subtract).then_inc(w16_rest_ready, 1)

            def twice(ap):
                return ap.unsqueeze(1).to_broadcast([P, PAIR, CHUNK])

            def whole(n, slot, in0, in1):
                wait(dve, prod_used, n - RING + 1)
                nc.vector.tensor_tensor(prod[:, slot % RING, :, :], in0, in1, ALU.mult).then_inc(prod_ready, 1)

            def products0(c, u):
                s = u % 2
                dve.wait_ge(x_base_loaded[s], (c - s + 2) * 8)
                if is_first(c):
                    dve.wait_ge(x_roll_loaded[s][0], 16)
                    nc.vector.tensor_tensor(prod[:, 0, 0, :], x_base[:, s, :], x_roll[:, s, 0, :], ALU.mult
                                            ).then_inc(first_tile_ready, 1)
                    dve.wait_ge(x_roll_loaded[s][1], 16)
                    nc.vector.tensor_tensor(prod[:, 0, 1, :], x_base[:, s, :], x_roll[:, s, 1, :], ALU.mult
                                            ).then_inc(prod_ready, 1)
                for k in range(1 if is_first(c) else 0, PAIRS0):
                    for b in range(k * PAIR, (k + 1) * PAIR):
                        dve.wait_ge(x_roll_loaded[s][b], (c - s + 2) * 8)
                    whole(first0(c) + k, slot0(c) + k, twice(x_base[:, s, :]), x_roll[:, s, k * PAIR:(k + 1) * PAIR, :])
                dve.wait_ge(x_part_loaded[s], (c - s + 2) * 16)
                wait(dve, lo16_ready, c)
                nc.vector.tensor_tensor(raw16[:, :], x_part[:, s, :], x_part16[:, s, :], ALU.mult
                                        ).then_inc(raw16_ready, 1)

            def split_rest16(c):
                dve.wait_ge(hi16_ready, c + 1)
                wait(dve, pairs16_used, c)
                nc.vector.tensor_tensor(lo16[:, :], raw16[:, :], hi16[:, :], ALU.subtract).then_inc(lo16_ready, 1)

            def split_product(c, u, b):
                s = u % 2
                if b == 0:
                    for a in range(PAIR, ROLLS):
                        dve.wait_ge(h1_rolled[s][a - 1], (c - s + 2) * 16)
                wait(dve, lo_ready, c * PAIRS1 + b)
                nc.vector.tensor_tensor(raw[:, :, :], h_roll[:, s, PAIR:2 * PAIR, :], twice(x_roll[:, s, b, :]),
                                        ALU.mult).then_inc(raw_ready, 1)

            def split_rest(c, b):
                dve.wait_ge(hi_ready, c * PAIRS1 + b + 1)
                slot = b % SPLIT_RING
                nc.vector.tensor_tensor(prod_lo[:, slot, :, :], raw[:, :, :], prod_hi[:, slot, :, :], ALU.subtract
                                        ).then_inc(lo_ready, 1)

            def layer2(c, u, group):
                dve.wait_ge(v_done, c + 1)
                dve.wait_ge(h2_ready, 2 * (c + 1))
                wait(dve, z2_done, group)
                nc.vector.tensor_tensor(h2v[:, u, :], v_ps[:, :], h2[:, u % 2, :], ALU.mult).then_inc(h2v_ready, 1)

            def sum_direct(c, u):
                dve.wait_ge(direct0_ready, c + 1)
                dve.wait_ge(direct1_ready, c + 1)
                nc.vector.tensor_reduce(top_a[:, bass.ds(c * ROWS, ROWS)],
                                        direct[:, u % 2, :].rearrange("p (r d) -> p r d", d=DIM),
                                        AX_X, ALU.add).then_inc(direct_summed, 1)

            def sum_z2(group):
                dve.wait_ge(z2_relu, group + 1)
                cols = BANK // DIM
                nc.vector.tensor_reduce(z2_sum[:, bass.ds(group * cols, cols)],
                                        z2_sb[:, :].rearrange("p (r d) -> p r d", d=DIM),
                                        AX_X, ALU.add).then_inc(z2_summed, 1)

            def step(c, u, group):
                s = u % 2
                if not is_last(c):
                    products0(c + 1, (u + 1) % UNROLL)
                dve.wait_ge(h1_ready, 2 * (c + 1))
                dve.wait_ge(h1_rolled[s][0], (c - s + 2) * 16)
                for b in range(ROLLS):
                    split_last = b == 0 and is_first(c)
                    if not split_last:
                        split_product(c, u, b)
                    if b == 0 and not is_last(c):
                        split_rest16(c + 1)
                    whole(first1(c) + b, slot1(c) + b, h_roll[:, s, 0:PAIR, :], twice(x_roll[:, s, b, :]))
                    if split_last:
                        split_product(c, u, b)
                    if b == 1 and not_first(c):
                        sum_direct(c - 1, (u - 1) % UNROLL)
                    split_rest(c, b)
                    if b == 1 and not_first(c):
                        layer2(c - 1, (u - 1) % UNROLL, group if u else group - 1)
                    if b == 3 and u == 1 and not_first(c, UNROLL):
                        sum_z2(group - 1)

            dve.wait_ge(w16_rest_placed, 16 * QUADS)
            nc.vector.tensor_copy(w16_sb[:, :, :], w16_raw).then_inc(w16_ready, 1)
            products0(0, 0)
            split_rest16(0)
            dve.wait_ge(w1_loaded, 48)
            nc.vector.tensor_copy(w1_hi[:, :, :], w1_raw).then_inc(w1_hi_ready, 1)
            dve.wait_ge(w1_hi_ready, 1)
            nc.vector.tensor_tensor(w1_lo[:, :, :], w1_raw, w1_hi[:, :, :], ALU.subtract).then_inc(w1_ready, 1)
            over_chunks(dve, step)
            layer2(CHUNKS - 1, UNROLL - 1, CHUNKS // UNROLL - 1)
            sum_direct(CHUNKS - 1, UNROLL - 1)
            sum_z2(CHUNKS // UNROLL - 1)
            dve.wait_ge(mlp_loaded, 16 * 7)
            dve.wait_ge(split_used, CHUNKS * PAIRS1)
            nc.vector.tensor_copy(wt2_hi, wt2_sb[:, :, :]).then_inc(wt2_hi_ready, 1)
            dve.wait_ge(wt2_hi_ready, 1)
            nc.vector.tensor_tensor(wt2_lo, wt2_sb[:, :, :], wt2_hi, ALU.subtract).then_inc(wt2_ready, 1)
            for n in range(BATCH_HALVES * M1):
                j, m = divmod(n, M1)
                cols = slice(j * BANK, (j + 1) * BANK)
                dve.wait_ge(mlp1_rounded, n + 1)
                nc.vector.tensor_tensor(mlp1_lo[:, m, cols], mlp1[:, m, cols], mlp1_hi[:, m, cols], ALU.subtract
                                        ).then_inc(mlp1_split, 1)
            n = BATCH_HALVES * (M1 + M2) + 1
            dve.wait_ge(mlp_done, n + 1)
            p = y_partition(1)
            nc.vector.tensor_copy(y_sb[p:p + 1, :], mlp_banks[n % len(mlp_banks)][p:p + 1, :]).then_inc(y_ready[1], 1)

        @block.tensor
        def _(pe):
            def mm(*args, **kw):
                return nc.tensor.matmul(*args, **kw)

            def over_banks(ps, weights, tile, start=False, stop=False):
                for j in range(CHUNK // BANK):
                    cols = slice(j * BANK, (j + 1) * BANK)
                    last = mm(ps[:, cols], weights, tile[:, cols], start=start, stop=stop)
                return last

            def whole(ps, n, slot, weights, start=False, stop=False):
                first = isinstance(n, int) and n == 0
                pe.wait_ge(first_tile_ready if first else prod_ready, 1 if first else n + 1)
                over_banks(ps, weights[:, 0, :], prod[:, slot % RING, 0, :], start=start)
                if first:
                    pe.wait_ge(prod_ready, 1)
                return over_banks(ps, weights[:, 1, :], prod[:, slot % RING, 1, :], stop=stop).then_inc(prod_used, 1)

            def split(ps, c, b, stop=False):
                pe.wait_ge(lo_ready, c * PAIRS1 + b + 1)
                slot = b % SPLIT_RING
                for k in range(PAIR):
                    t = b * PAIR + k
                    over_banks(ps, w1_hi[:, t, :], prod_hi[:, slot, k, :])
                    over_banks(ps, w1_hi[:, t, :], prod_lo[:, slot, k, :])
                    last = over_banks(ps, w1_lo[:, t, :], prod_hi[:, slot, k, :], stop=stop and k == PAIR - 1)
                return last.then_inc(split_used, 1)

            def layer0(c, u):
                wait(pe, h1_ready, 2 * c)
                wait(pe, direct0_ready, c)
                for k in range(PAIRS0):
                    whole(z0_ps, first0(c) + k, slot0(c) + k, w0_sb[:, k * PAIR:(k + 1) * PAIR, :], start=k == 0)

            def layer0_pairs16(c):
                pe.wait_ge(lo16_ready, c + 1)
                for q in range(QUADS):
                    cols = slice(q * PART, (q + 1) * PART)
                    mm(z0_ps[:, cols], w16_sb[:, q, :], hi16[:, :], start=False, stop=False)
                    last = mm(z0_ps[:, cols], w16_sb[:, q, :], lo16[:, :], start=False,
                              stop=(q + 1) * PART % BANK == 0)
                last.then_inc(pairs16_used, 1)

            def layer2_v(c, u):
                wait(pe, h2v_ready, c)
                for q in range(QUADS):
                    half, at = divmod(q * PART, BANK)
                    last = mm(v_ps[half * HID:(half + 1) * HID, at:at + PART], w2_sb[:, q, :],
                              x_part[:, u % 2, :], start=True, stop=True)
                last.then_inc(v_done, 1)

            def layer2_sum(h2v_count, z2_relu_count):
                pe.wait_ge(h2v_ready, h2v_count)
                wait(pe, z2_relu, z2_relu_count)
                for u in range(UNROLL):
                    last = mm(z2_ps[FIELDS * u:FIELDS * (u + 1), :], half_ones[:, :], h2v[:, u, :],
                              start=True, stop=True)
                last.then_inc(z2_done, 1)

            def step(c, u, group):
                if not is_last(c):
                    layer0(c + 1, (u + 1) % UNROLL)
                    layer0_pairs16(c + 1)
                wait(pe, h2_ready, 2 * c)
                wait(pe, direct1_ready, c)
                for b in range(ROLLS):
                    whole(z1_ps, first1(c) + b, slot1(c) + b, w1_sb[:, b * PAIR:(b + 1) * PAIR, :], start=b == 0)
                    split(z1_ps, c, b, stop=b == ROLLS - 1)
                    if b == 1:
                        layer2_v(c, u)
                    if b == 2 and u == 0 and not_first(c):
                        layer2_sum(c, group - 1)

            pe.wait_ge(w0_ready, 1)
            layer0(0, 0)
            pe.wait_ge(w16_ready, 1)
            layer0_pairs16(0)
            pe.wait_ge(w1_ready, 1)
            pe.wait_ge(ones_ready, 2)
            over_chunks(pe, step)

            banks = len(mlp_banks)

            def free_bank(n):
                wait(pe, mlp_relu, n - banks + 1)
                return mlp_banks[n % banks]

            def top1_a(n):
                j, m = divmod(n, M1)
                mm(free_bank(n), wt1a_sb[:, m * P:(m + 1) * P], top_a[:, j * BANK:(j + 1) * BANK],
                   start=True, stop=False)

            def top1_b(n):
                j, m = divmod(n, M1)
                mm(mlp_banks[n % banks], wt1b_sb[:, m * P:(m + 1) * P], top_b[:, j * BANK:(j + 1) * BANK],
                   start=False, stop=True).then_inc(mlp_done, 1)

            pe.wait_ge(mlp_loaded, 16 * 7)
            pe.wait_ge(direct0_ready, CHUNKS)
            pe.wait_ge(h1_ready, 2 * CHUNKS)
            pe.wait_ge(direct_summed, CHUNKS // BATCH_HALVES)
            pe.wait_ge(z2_row[0], 16 * 2 * UNROLL)
            for n in range(M1):
                if n == M1 // 2:
                    layer2_sum(CHUNKS, CHUNKS // UNROLL - 1)
                top1_a(n)
                top1_b(n)
            pe.wait_ge(h2_ready, 2 * CHUNKS)
            pe.wait_ge(direct_summed, CHUNKS)
            for n in range(M1, 2 * M1):
                top1_a(n)
            pe.wait_ge(z2_row[1], 16 * 2 * UNROLL)
            for n in range(M1, 2 * M1):
                top1_b(n)
            n = BATCH_HALVES * M1
            pe.wait_ge(wt2_ready, 1)
            for j in range(BATCH_HALVES):
                cols = slice(j * BANK, (j + 1) * BANK)
                for m in range(M2):
                    to = free_bank(n)
                    outs = slice(m * P, (m + 1) * P)
                    for k in range(M1):
                        pe.wait_ge(mlp1_split, j * M1 + k + 1)
                        mm(to, wt2_hi[:, k, outs], mlp1_hi[:, k, cols], start=k == 0, stop=False)
                        mm(to, wt2_hi[:, k, outs], mlp1_lo[:, k, cols], start=False, stop=False)
                        last = mm(to, wt2_lo[:, k, outs], mlp1_hi[:, k, cols], start=False, stop=k == M1 - 1)
                    last.then_inc(mlp_done, 1)
                    n += 1
            to = [free_bank(n + j) for j in range(BATCH_HALVES)]
            for k in range(M2):
                pe.wait_ge(mlp_relu, BATCH_HALVES * M1 + (BATCH_HALVES - 1) * M2 + k + 1)
                for j in range(BATCH_HALVES):
                    p = y_partition(j)
                    last = mm(to[j][p:p + 1, :], wt3_sb[:, k:k + 1], mlp2[:, k, j * BANK:(j + 1) * BANK],
                              start=k == 0, stop=k == M2 - 1)
                    if k == M2 - 1:
                        last.then_inc(mlp_done, 1)

        @block.scalar
        def _(act):
            act.dma_start(base_sb[:, :], row_base).then_inc(ids_loaded, 16)
            act.dma_start(b0_sb[:, :], b0).then_inc(biases_loaded, 16)
            act.dma_start(w0_sb[:, :, :], w0[:, 0:ROLLS, :]).then_inc(w0_loaded, 16)
            act.dma_start(w0_swap, w0_swapped[:, 0:ROLLS, :]).then_inc(w0_loaded, 16)
            act.dma_start(w16_raw, w0[:, ROLLS:, :]).then_inc(w16_loaded, 16)
            act.dma_start(w16_swap, w0_swapped[:, ROLLS:, :]).then_inc(w16_loaded, 16)
            act.dma_start(b1_sb[:, :], b1).then_inc(biases_loaded, 16)
            act.dma_start(b2_sb[:, :], b2).then_inc(biases_loaded, 16)
            act.dma_start(w1_raw, w1_split).then_inc(w1_loaded, 16)
            act.dma_start(w1_sb[:, :, :], w1_whole).then_inc(w1_loaded, 16)
            act.dma_start(w2_sb[:, :, :], w2).then_inc(w1_loaded, 16)
            act.dma_start(wt1a_sb[:, :], wt1a).then_inc(mlp_loaded, 16)
            act.dma_start(wt1b_sb[:, :], wt1b).then_inc(mlp_loaded, 16)
            act.dma_start(wt2_sb[:, :, :], wt2).then_inc(mlp_loaded, 16)
            act.dma_start(wt3_sb[:, :], wt3).then_inc(mlp_loaded, 16)
            act.dma_start(bt1_sb[:, :], bt1).then_inc(mlp_loaded, 16)
            act.dma_start(bt2_sb[:, :], bt2).then_inc(mlp_loaded, 16)
            act.wait_ge(top_b_zeroed, 1)
            act.dma_start(top_b[1:1 + DENSE, :], dense_t).then_inc(mlp_loaded, 16)

            def relu0(c, u):
                s = u % 2
                act.wait_ge(pairs16_used, c + 1)
                if not_first(c, 2):
                    act.wait_ge(prod_ready, first1(c - 2) + PAIRS1)
                for half in range(2):
                    nc.scalar.activation(h_roll[half * HID:(half + 1) * HID, s, 0, :], z0_ps[0:HID, :], ACT.Relu,
                                         bias=b0_sb[0:HID, :]).then_inc(h1_ready, 1)
                wait(act, direct_summed, c - 1)
                nc.scalar.activation(direct[0:HID, s, :], z0_ps[HID:P, :], ACT.Relu,
                                     bias=b0_sb[HID:P, :]).then_inc(direct0_ready, 1)
                act.wait_ge(h1_ready, 2 * (c + 1))
                for a in range(1, ROLLS):
                    r = H_ROLL * a
                    act.dma_start(h_roll[0:P - r, s, a, :], h_roll[r:P, s, 0, :]).then_inc(h1_rolled[s][a - 1], 16)
                    act.dma_start(h_roll[P - r:P, s, a, :], h_roll[0:r, s, 0, :]).then_inc(h1_rolled[s][a - 1], 16)

            def relu1(c, u):
                s = u % 2
                act.wait_ge(split_used, (c + 1) * PAIRS1)
                wait(act, h2v_ready, c - 1)
                for half in range(2):
                    nc.scalar.activation(h2[half * HID:(half + 1) * HID, s, :],
                                         z1_ps[0:HID, half * BANK:(half + 1) * BANK], ACT.Relu,
                                         bias=b1_sb[0:HID, :]).then_inc(h2_ready, 1)
                nc.scalar.activation(direct[HID:P, s, :], z1_ps[HID:P, :], ACT.Relu,
                                     bias=b1_sb[HID:P, :]).then_inc(direct1_ready, 1)

            def relu2(done, summed):
                act.wait_ge(z2_done, done)
                wait(act, z2_summed, summed)
                nc.scalar.activation(z2_sb[:, :], z2_ps[:, :], ACT.Relu, bias=b2_sb[:, :]).then_inc(z2_relu, 1)

            def round_products(c, b):
                act.wait_ge(raw_ready, c * PAIRS1 + b + 1)
                wait(act, split_used, c * PAIRS1 + b + 1 - SPLIT_RING)
                nc.scalar.copy(prod_hi[:, b % SPLIT_RING, :, :], raw[:, :, :]).then_inc(hi_ready, 1)

            def round_pairs16(c):
                act.wait_ge(raw16_ready, c + 1)
                wait(act, pairs16_used, c)
                nc.scalar.copy(hi16[:, :], raw16[:, :]).then_inc(hi16_ready, 1)

            def step(c, u, group):
                if not is_last(c):
                    round_pairs16(c + 1)
                round_products(c, 0)
                if not_first(c):
                    relu1(c - 1, (u - 1) % UNROLL)
                round_products(c, 1)
                if not is_last(c):
                    relu0(c + 1, (u + 1) % UNROLL)
                round_products(c, 2)
                round_products(c, 3)
                if u == 0 and not_first(c):
                    relu2(group, group - 1)

            act.wait_ge(biases_loaded, 48)
            nc.scalar.activation(table_warm[:, :], b0_sb[:, :], ACT.Relu)
            act.wait_ge(w16_rest_ready, 1)
            for q in range(QUADS):
                rows = slice(q * FIELDS + FIELDS // 2, (q + 1) * FIELDS)
                act.dma_start(w16_raw[rows, q, :], w16_rest[rows, q, :]).then_inc(w16_rest_placed, 16)
            round_pairs16(0)
            relu0(0, 0)
            over_chunks(act, step)
            relu1(CHUNKS - 1, UNROLL - 1)

            def relu_mlp(n, to, bias):
                act.wait_ge(mlp_done, n + 1)
                nc.scalar.activation(to, mlp_banks[n % len(mlp_banks)], ACT.Relu, bias=bias).then_inc(mlp_relu, 1)

            act.wait_ge(mlp_loaded, 16 * 7)
            act.wait_ge(prod_ready, first1(CHUNKS - 1) + PAIRS1)
            def round_mlp1(n):
                j, m = divmod(n, M1)
                cols = slice(j * BANK, (j + 1) * BANK)
                act.wait_ge(mlp_relu, n + 1)
                nc.scalar.copy(mlp1_hi[:, m, cols], mlp1[:, m, cols]).then_inc(mlp1_rounded, 1)

            act.wait_ge(split_used, CHUNKS * PAIRS1)
            for n in range(BATCH_HALVES * M1):
                if n == M1 // 2:
                    relu2(CHUNKS // UNROLL, CHUNKS // UNROLL - 1)
                j, m = divmod(n, M1)
                relu_mlp(n, mlp1[:, m, j * BANK:(j + 1) * BANK], bt1_sb[:, m:m + 1])
                if n == M1 // 2:
                    act.wait_ge(z2_summed, CHUNKS // UNROLL)
                    for u in range(UNROLL):
                        row_of_z2(act, BATCH_HALVES - 1, u, 0)
                if n > 0:
                    round_mlp1(n - 1)
            round_mlp1(BATCH_HALVES * M1 - 1)
            for j in range(BATCH_HALVES):
                for m in range(M2):
                    n = BATCH_HALVES * M1 + j * M2 + m
                    relu_mlp(n, mlp2[:, m, j * BANK:(j + 1) * BANK], bt2_sb[:, m:m + 1])
            n = BATCH_HALVES * (M1 + M2)
            act.wait_ge(mlp_done, n + 1)
            nc.scalar.copy(y_sb[0:1, :], mlp_banks[n % len(mlp_banks)][0:1, :]).then_inc(y_ready[0], 1)
            for j in range(BATCH_HALVES):
                act.wait_ge(y_ready[j], 1)
                p = y_partition(j)
                act.dma_start(out[j * BANK:(j + 1) * BANK, :].rearrange("b o -> o b"), y_sb[p:p + 1, :]
                              ).then_inc(y_stored, 16)
            act.wait_ge(y_stored, 16 * BATCH_HALVES)


def lay_out(inputs):
    import numpy as np
    a = {k: np.asarray(v) for k, v in inputs.items()}
    tables = [a[f"tbl_{f}"] for f in range(FIELDS)]
    first_row = np.cumsum([0] + [t.shape[0] for t in tables[:-1]]).astype(np.int32)
    r = np.arange(P)
    quad, i = r // FIELDS, r % FIELDS

    arrays = {"table": np.concatenate(tables, axis=0)}
    arrays["gather_ids"] = a["ids"].reshape(CHUNKS, QUADS, GATHERS, FIELDS).transpose(1, 3, 0, 2).reshape(P, -1)
    arrays["row_base"] = np.repeat(first_row[i][:, None], UNROLL * GATHERS, axis=1)

    w0 = a["L0_rec_W0"].reshape(P, FIELDS, FIELDS)
    w0_tiles = np.zeros((P, ROLLS + QUADS, P), w0.dtype)
    w0_swapped = np.zeros_like(w0_tiles)
    for b in range(ROLLS):
        j = (i + x_shift(quad, b)) % FIELDS
        w0_tiles[:, b, :] = w0[:, i, j].T
        keep = r[i != j]
        w0_swapped[keep, b, :] = w0[:, j[keep], i[keep]].T
    low = np.arange(FIELDS // 2)
    for q in range(QUADS):
        for rows in (q * FIELDS + low, q * FIELDS + low + FIELDS // 2):
            w0_tiles[rows, ROLLS + q, :] = w0[:, low, low + FIELDS // 2].T
            w0_swapped[rows, ROLLS + q, :] = w0[:, low + FIELDS // 2, low].T
    arrays["w0"], arrays["w0_swapped"] = w0_tiles, w0_swapped

    w1 = a["L0_rec_W1"].reshape(P, HID, FIELDS)
    for name, copies in (("w1_whole", range(0, PAIR)), ("w1_split", range(PAIR, ROLLS))):
        arrays[name] = np.stack([w1[:, (r + H_ROLL * k) % HID, (i + x_shift(quad, b)) % FIELDS].T
                                 for b in range(ROLLS) for k in copies], axis=1)
    w2 = a["L0_rec_W2"].reshape(HID, FIELDS)
    w2_tiles = np.zeros((P, QUADS, HID), w2.dtype)
    for q in range(QUADS):
        w2_tiles[q * FIELDS:(q + 1) * FIELDS, q, :] = w2.T
    arrays["w2"] = w2_tiles
    arrays["b0"], arrays["b1"] = a["L0_rec_b0"][:, None], a["L0_rec_b1"][:, None]
    arrays["b2"] = np.repeat(a["L0_rec_b2"][:, None], P, axis=0)
    arrays["dense_t"] = a["dense_ctx"].T
    arrays["wt1a"] = a["W_top1"][:P]
    arrays["wt1b"] = np.pad(a["W_top1"][P:], ((0, P - 1 - DENSE), (0, 0)))
    arrays["bt1"] = a["b_top1"].reshape(M1, P).T
    arrays["wt2"] = a["W_top2"].reshape(M1, P, TOP2).transpose(1, 0, 2)
    arrays["bt2"] = a["b_top2"].reshape(M2, P).T
    arrays["wt3"] = a["W_top3"].reshape(M2, P).T
    return {k: np.ascontiguousarray(v) for k, v in arrays.items()}


_ORDER = ["gather_ids", "row_base", "table", "w0", "w0_swapped", "w1_whole", "w1_split", "w2", "b0", "b1", "b2",
          "dense_t", "wt1a", "wt1b", "bt1", "wt2", "bt2", "wt3"]


def kernel(**inputs):
    import numpy as _np
    import concourse.bacc as _bacc
    from concourse import mybir as _mybir
    from concourse.bass_utils import run_bass_kernel_spmd as _run

    nc = _bacc.Bacc("TRN2", target_bir_lowering=False, num_devices=1)
    laid = lay_out(inputs)
    arrays, args = {}, []
    for name in _ORDER:
        arrays[f"in_{name}"] = laid[name]
        args.append(nc.dram_tensor(f"in_{name}", laid[name].shape, _mybir.dt.from_np(laid[name].dtype),
                                   kind="ExternalInput").ap())
    out = nc.dram_tensor("out_y", (BATCH, 1), _mybir.dt.from_np(_np.dtype("float32")), kind="ExternalOutput").ap()
    build_tower(nc, *args, out)
    r = _run(nc, [arrays], core_ids=[0])
    return r.results[0]["out_y"]
```
